# Optimizing a Trainium2 kernel written in Bass

```python
import numpy as np
import jax
import jax.numpy as jnp

def _softmax(x, axis=-1):
    return jax.nn.softmax(x, axis=axis)

def _gelu(x):
    return jax.nn.gelu(x, approximate=True)

def _silu(x):
    return jax.nn.silu(x)

def _sigmoid(x):
    return jax.nn.sigmoid(x)

def _layernorm(x, axis=-1, eps=1e-05):
    m = jnp.mean(x, axis=axis, keepdims=True)
    v = jnp.var(x, axis=axis, keepdims=True)
    return (x - m) / jnp.sqrt(v + eps)

def _scatter_add(tgt, idx, src, axis=0):
    return tgt.at[idx].add(src)

def _segment_sum(src, seg, n):
    return jax.ops.segment_sum(src, seg, n)
kernel_name = 'mk_gnn_resnorm_d4_gnn_r32_24d957'

def setup_inputs(seed: int=0):
    np.random.seed(seed)
    _w = jnp.asarray

    def _rec_inputs():
        import jax
        import jax.numpy as jnp
        _gk = jax.random.key(seed)
        x = -0.000202 + 1 * jax.random.normal(jax.random.fold_in(_gk, 1), (3125, 64), jnp.float32)
        _s = jax.random.randint(jax.random.fold_in(_gk, 2), (50000,), 0, 3125, jnp.int32)
        _d = jax.random.randint(jax.random.fold_in(_gk, 3), (50000,), 0, 3125, jnp.int32)
        _loop = jnp.arange(3125, dtype=jnp.int32)
        src = jnp.concatenate([_s, _d, _loop])
        dst = jnp.concatenate([_d, _s, _loop])
        _o = jnp.argsort(dst, stable=True)
        src = src[_o]
        dst = dst[_o]
        edge_attr_32 = 0.000102155 + 1.00015 * jax.random.normal(jax.random.fold_in(_gk, 12), (103125, 32), jnp.float32)
        edge_type_8 = jax.random.randint(jax.random.fold_in(_gk, 14), (103125,), 0, 8, jnp.int32)
        edge_weight = jax.random.uniform(jax.random.fold_in(_gk, 15), (103125,), jnp.float32, 0.0, 1)
        edge_weight1 = 0.000614103 + 0.999867 * jax.random.normal(jax.random.fold_in(_gk, 16), (103125, 1), jnp.float32)
        return (x, src, dst, edge_attr_32, edge_type_8, edge_weight, edge_weight1)
    x, src, dst, edge_attr_32, edge_type_8, edge_weight, edge_weight1 = _rec_inputs()

    def _L0_gnn_setup():
        import jax, jax.numpy as jnp
        import numpy as np
        N = 3125
        E = 50000
        D = 64
        EPS = 1e-12
        key = jax.random.key(seed)
        k1, k2, k3 = jax.random.split(key, 3)
        H = jax.random.normal(k1, (N, D), dtype=jnp.float32)
        row = jnp.sort(jax.random.randint(k2, (E,), 0, N, dtype=jnp.int64))
        col = jax.random.randint(k3, (E,), 0, N, dtype=jnp.int64)
        return {'H': H, 'row': row, 'col': col, 'num_nodes': N}
    _L0_gnn_all = _L0_gnn_setup()
    _L0_gnn_in = {k: v for k, v in _L0_gnn_all.items() if k in ()}
    del _L0_gnn_all

    def _L1_gnn_setup():
        import jax, jax.numpy as jnp
        import numpy as np
        N_NODES = 3125
        N_EDGES = 31250
        NODE_DIM = 64
        EDGE_DIM = 32
        HIDDEN = 64

        def _unif(key, shape, fan_in):
            bound = 1.0 / np.sqrt(fan_in)
            return jax.random.uniform(key, shape, jnp.float32, -bound, bound)
        key = jax.random.key(seed)
        ks = jax.random.split(key, 11)
        node_features = jax.random.normal(ks[0], (N_NODES, NODE_DIM), jnp.float32)
        edge_index = jax.random.randint(ks[1], (2, N_EDGES), 0, N_NODES, dtype=jnp.int64)
        edge_features = jax.random.normal(ks[2], (N_EDGES, EDGE_DIM), jnp.float32)
        in_dim = 2 * NODE_DIM + EDGE_DIM
        W1 = _unif(ks[3], (HIDDEN, in_dim), in_dim)
        b1 = _unif(ks[4], (HIDDEN,), in_dim)
        W2 = _unif(ks[5], (HIDDEN, HIDDEN), HIDDEN)
        b2 = _unif(ks[6], (HIDDEN,), HIDDEN)
        w_ih = _unif(ks[7], (3 * NODE_DIM, HIDDEN), NODE_DIM)
        w_hh = _unif(ks[8], (3 * NODE_DIM, NODE_DIM), NODE_DIM)
        b_ih = _unif(ks[9], (3 * NODE_DIM,), NODE_DIM)
        b_hh = _unif(ks[10], (3 * NODE_DIM,), NODE_DIM)
        return {'node_features': node_features, 'edge_index': edge_index, 'edge_features': edge_features, 'W1': W1, 'b1': b1, 'W2': W2, 'b2': b2, 'w_ih': w_ih, 'w_hh': w_hh, 'b_ih': b_ih, 'b_hh': b_hh}
    _L1_gnn_all = _L1_gnn_setup()
    _L1_gnn_in = {k: v for k, v in _L1_gnn_all.items() if k in ('W1', 'b1', 'W2', 'b2', 'w_ih', 'w_hh', 'b_ih', 'b_hh')}
    del _L1_gnn_all

    def _L2_gnn_setup():
        import jax, jax.numpy as jnp
        import numpy as np
        N_NODES = 3125
        N_EDGES = 100000
        N_RELS = 8
        F_IN = 64
        F_OUT = 64
        key = jax.random.key(seed)
        k1, k2, k3, k4, k5, k6 = jax.random.split(key, 6)
        X = jax.random.normal(k1, (N_NODES, F_IN), dtype=jnp.float32)
        W = jax.random.normal(k2, (N_RELS, F_IN, F_OUT), dtype=jnp.float32) * 0.1
        A = jax.random.uniform(k3, (N_EDGES,), dtype=jnp.float32)
        src = jax.random.randint(k4, (N_EDGES,), 0, N_NODES, dtype=jnp.int32)
        dst = jax.random.randint(k5, (N_EDGES,), 0, N_NODES, dtype=jnp.int32)
        etype = jax.random.randint(k6, (N_EDGES,), 0, N_RELS, dtype=jnp.int32)
        return {'X': X, 'W': W, 'A': A, 'src': src, 'dst': dst, 'etype': etype}
    _L2_gnn_all = _L2_gnn_setup()
    _L2_gnn_in = {k: v for k, v in _L2_gnn_all.items() if k in ('W',)}
    del _L2_gnn_all

    def _L3_gnn_setup():
        import jax, jax.numpy as jnp
        import numpy as np
        N, E, D_IN, D_H, D_OUT = (50000, 25000, 64, 64, 64)

        def _lin_params(key, d_in, d_out, bias=True, scale=0.05):
            kw, kb = jax.random.split(key)
            W = jax.random.normal(kw, (d_in, d_out), dtype=jnp.float32) * scale
            if bias:
                b = jax.random.normal(kb, (d_out,), dtype=jnp.float32) * scale
                return (W, b)
            return (W,)

        def transformer_conv(x, src, dst, edge_attr, Wq, bq, Wk, bk, Wv, bv, We, Ws, bs):
            d = Wq.shape[1]
            n = x.shape[0]
            q = x @ Wq + bq
            e = edge_attr @ We
            k = x[src] @ Wk + bk + e
            v = x[src] @ Wv + bv + e
            score = jnp.sum(q[dst] * k, axis=-1) / jnp.sqrt(jnp.asarray(d, x.dtype))
            m = jax.ops.segment_max(score, dst, num_segments=n)
            a = jnp.exp(score - m[dst])
            denom = jax.ops.segment_sum(a, dst, num_segments=n)
            alpha = a / denom[dst]
            out = jax.ops.segment_sum(alpha[:, None] * v, dst, num_segments=n)
            return out + x @ Ws + bs
        key = jax.random.key(seed)
        ks = jax.random.split(key, 12)
        x = jax.random.normal(ks[0], (N, D_IN), dtype=jnp.float32)
        edge_index = jax.random.randint(ks[1], (2, E), 0, N, dtype=jnp.int64)
        edge_attr = jax.random.normal(ks[2], (E, 1), dtype=jnp.float32)
        Wq1, bq1 = _lin_params(ks[3], D_IN, D_H)
        Wk1, bk1 = _lin_params(ks[4], D_IN, D_H)
        Wv1, bv1 = _lin_params(ks[5], D_IN, D_H)
        We1, = _lin_params(ks[6], 1, D_H, bias=False)
        Ws1, bs1 = _lin_params(ks[7], D_IN, D_H)
        Wq2, bq2 = _lin_params(ks[8], D_H, D_OUT)
        Wk2, bk2 = _lin_params(ks[9], D_H, D_OUT)
        Wv2, bv2 = _lin_params(ks[10], D_H, D_OUT)
        We2, = _lin_params(jax.random.fold_in(key, 100), 1, D_OUT, bias=False)
        Ws2, bs2 = _lin_params(ks[11], D_H, D_OUT)
        return dict(x=x, edge_index=edge_index, edge_attr=edge_attr, Wq1=Wq1, bq1=bq1, Wk1=Wk1, bk1=bk1, Wv1=Wv1, bv1=bv1, We1=We1, Ws1=Ws1, bs1=bs1, Wq2=Wq2, bq2=bq2, Wk2=Wk2, bk2=bk2, Wv2=Wv2, bv2=bv2, We2=We2, Ws2=Ws2, bs2=bs2)
    _L3_gnn_all = _L3_gnn_setup()
    _L3_gnn_in = {k: v for k, v in _L3_gnn_all.items() if k in ('Wq1', 'bq1', 'Wk1', 'bk1', 'Wv1', 'bv1', 'We1', 'Ws1', 'bs1', 'Wq2', 'bq2', 'Wk2', 'bk2', 'Wv2', 'bv2', 'We2', 'Ws2', 'bs2')}
    del _L3_gnn_all
    return {'x': x, 'src': src, 'dst': dst, 'edge_attr_32': edge_attr_32, 'edge_type_8': edge_type_8, 'edge_weight': edge_weight, 'edge_weight1': edge_weight1, 'L1_gnn_W1': _L1_gnn_in['W1'], 'L1_gnn_b1': _L1_gnn_in['b1'], 'L1_gnn_W2': _L1_gnn_in['W2'], 'L1_gnn_b2': _L1_gnn_in['b2'], 'L1_gnn_w_ih': _L1_gnn_in['w_ih'], 'L1_gnn_w_hh': _L1_gnn_in['w_hh'], 'L1_gnn_b_ih': _L1_gnn_in['b_ih'], 'L1_gnn_b_hh': _L1_gnn_in['b_hh'], 'L2_gnn_W': _L2_gnn_in['W'], 'L3_gnn_Wq1': _L3_gnn_in['Wq1'], 'L3_gnn_bq1': _L3_gnn_in['bq1'], 'L3_gnn_Wk1': _L3_gnn_in['Wk1'], 'L3_gnn_bk1': _L3_gnn_in['bk1'], 'L3_gnn_Wv1': _L3_gnn_in['Wv1'], 'L3_gnn_bv1': _L3_gnn_in['bv1'], 'L3_gnn_We1': _L3_gnn_in['We1'], 'L3_gnn_Ws1': _L3_gnn_in['Ws1'], 'L3_gnn_bs1': _L3_gnn_in['bs1'], 'L3_gnn_Wq2': _L3_gnn_in['Wq2'], 'L3_gnn_bq2': _L3_gnn_in['bq2'], 'L3_gnn_Wk2': _L3_gnn_in['Wk2'], 'L3_gnn_bk2': _L3_gnn_in['bk2'], 'L3_gnn_Wv2': _L3_gnn_in['Wv2'], 'L3_gnn_bv2': _L3_gnn_in['bv2'], 'L3_gnn_We2': _L3_gnn_in['We2'], 'L3_gnn_Ws2': _L3_gnn_in['Ws2'], 'L3_gnn_bs2': _L3_gnn_in['bs2']}

def reference(x, src, dst, edge_attr_32, edge_type_8, edge_weight, edge_weight1, L1_gnn_W1, L1_gnn_b1, L1_gnn_W2, L1_gnn_b2, L1_gnn_w_ih, L1_gnn_w_hh, L1_gnn_b_ih, L1_gnn_b_hh, L2_gnn_W, L3_gnn_Wq1, L3_gnn_bq1, L3_gnn_Wk1, L3_gnn_bk1, L3_gnn_Wv1, L3_gnn_bv1, L3_gnn_We1, L3_gnn_Ws1, L3_gnn_bs1, L3_gnn_Wq2, L3_gnn_bq2, L3_gnn_Wk2, L3_gnn_bk2, L3_gnn_Wv2, L3_gnn_bv2, L3_gnn_We2, L3_gnn_Ws2, L3_gnn_bs2):
    import jax
    import jax.numpy as jnp

    def _L0_gnn_ref(H, row, col, num_nodes):
        import jax, jax.numpy as jnp
        import numpy as np
        N = 3125
        E = 50000
        D = 64
        EPS = 1e-12
        norm = jnp.sqrt(jnp.sum(H * H, axis=1, keepdims=True))
        Hn = H / jnp.maximum(norm, EPS)
        scores = jnp.sum(Hn[row] * Hn[col], axis=1)
        m = jax.ops.segment_max(scores, row, num_segments=num_nodes)
        e = jnp.exp(scores - m[row])
        s = jax.ops.segment_sum(e, row, num_segments=num_nodes)
        attn = e / s[row]
        out = jax.ops.segment_sum(attn[:, None] * H[col], row, num_segments=num_nodes)
        return out

    def _L1_gnn_ref(node_features, edge_index, edge_features, W1, b1, W2, b2, w_ih, w_hh, b_ih, b_hh):
        import jax, jax.numpy as jnp
        import numpy as np
        N_NODES = 3125
        N_EDGES = 31250
        NODE_DIM = 64
        EDGE_DIM = 32
        HIDDEN = 64

        def _unif(key, shape, fan_in):
            bound = 1.0 / np.sqrt(fan_in)
            return jax.random.uniform(key, shape, jnp.float32, -bound, bound)
        src, dst = (edge_index[0], edge_index[1])
        x = jnp.concatenate([node_features[src], node_features[dst], edge_features], axis=-1)
        h = jax.nn.relu(x @ W1.T + b1)
        messages = h @ W2.T + b2
        agg = jax.ops.segment_sum(messages, dst, num_segments=node_features.shape[0])
        gi = agg @ w_ih.T + b_ih
        gh = node_features @ w_hh.T + b_hh
        i_r, i_z, i_n = jnp.split(gi, 3, axis=-1)
        h_r, h_z, h_n = jnp.split(gh, 3, axis=-1)
        r = jax.nn.sigmoid(i_r + h_r)
        z = jax.nn.sigmoid(i_z + h_z)
        n = jnp.tanh(i_n + r * h_n)
        return (1.0 - z) * n + z * node_features

    def _L2_gnn_ref(X, W, A, src, dst, etype):
        import jax, jax.numpy as jnp
        import numpy as np
        N_NODES = 3125
        N_EDGES = 100000
        N_RELS = 8
        F_IN = 64
        F_OUT = 64
        XW = jnp.einsum('nf,rfo->rno', X, W)
        msg = XW[etype, src] * A[:, None]
        Y = jax.ops.segment_sum(msg, dst, num_segments=X.shape[0])
        return Y

    def _L3_gnn_ref(x, edge_index, edge_attr, Wq1, bq1, Wk1, bk1, Wv1, bv1, We1, Ws1, bs1, Wq2, bq2, Wk2, bk2, Wv2, bv2, We2, Ws2, bs2):
        import jax, jax.numpy as jnp
        import numpy as np
        N, E, D_IN, D_H, D_OUT = (50000, 25000, 64, 64, 64)

        def _lin_params(key, d_in, d_out, bias=True, scale=0.05):
            kw, kb = jax.random.split(key)
            W = jax.random.normal(kw, (d_in, d_out), dtype=jnp.float32) * scale
            if bias:
                b = jax.random.normal(kb, (d_out,), dtype=jnp.float32) * scale
                return (W, b)
            return (W,)

        def transformer_conv(x, src, dst, edge_attr, Wq, bq, Wk, bk, Wv, bv, We, Ws, bs):
            d = Wq.shape[1]
            n = x.shape[0]
            q = x @ Wq + bq
            e = edge_attr @ We
            k = x[src] @ Wk + bk + e
            v = x[src] @ Wv + bv + e
            score = jnp.sum(q[dst] * k, axis=-1) / jnp.sqrt(jnp.asarray(d, x.dtype))
            m = jax.ops.segment_max(score, dst, num_segments=n)
            a = jnp.exp(score - m[dst])
            denom = jax.ops.segment_sum(a, dst, num_segments=n)
            alpha = a / denom[dst]
            out = jax.ops.segment_sum(alpha[:, None] * v, dst, num_segments=n)
            return out + x @ Ws + bs
        src, dst = (edge_index[0], edge_index[1])
        h = transformer_conv(x, src, dst, edge_attr, Wq1, bq1, Wk1, bk1, Wv1, bv1, We1, Ws1, bs1)
        h = jax.nn.relu(h)
        out = transformer_conv(h, src, dst, edge_attr, Wq2, bq2, Wk2, bk2, Wv2, bv2, We2, Ws2, bs2)
        return out
    edge_index = jnp.stack([src, dst])
    x = _layernorm(x + _L0_gnn_ref(x, src, dst, 3125), axis=-1)
    x = _layernorm(x + _L1_gnn_ref(x, edge_index, edge_attr_32, L1_gnn_W1, L1_gnn_b1, L1_gnn_W2, L1_gnn_b2, L1_gnn_w_ih, L1_gnn_w_hh, L1_gnn_b_ih, L1_gnn_b_hh), axis=-1)
    x = _layernorm(x + _L2_gnn_ref(x, L2_gnn_W, edge_weight, src, dst, edge_type_8), axis=-1)
    x = _layernorm(x + _L3_gnn_ref(x, edge_index, edge_weight1, L3_gnn_Wq1, L3_gnn_bq1, L3_gnn_Wk1, L3_gnn_bk1, L3_gnn_Wv1, L3_gnn_bv1, L3_gnn_We1, L3_gnn_Ws1, L3_gnn_bs1, L3_gnn_Wq2, L3_gnn_bq2, L3_gnn_Wk2, L3_gnn_bk2, L3_gnn_Wv2, L3_gnn_bv2, L3_gnn_We2, L3_gnn_Ws2, L3_gnn_bs2), axis=-1)
    return x

_drawn_inputs = setup_inputs


def setup_inputs(seed=0):
    import zlib

    import numpy as np

    out = dict(_drawn_inputs(seed))
    spreads = {}
    factors = {'edge_weight1': 6.68,
     'L1_gnn_b_ih': 3.642,
     'L1_gnn_b_hh': 4.788,
     'L3_gnn_Wq1': 8.0,
     'L3_gnn_bq1': 8.0,
     'L3_gnn_Wk1': 8.0,
     'L3_gnn_bk1': 64.0,
     'L3_gnn_bv1': 3.034,
     'L3_gnn_We1': 8.0,
     'L3_gnn_bs1': 2.932,
     'L3_gnn_Wq2': 8.0,
     'L3_gnn_bq2': 8.0,
     'L3_gnn_Wk2': 8.0,
     'L3_gnn_bk2': 64.0,
     'L3_gnn_We2': 6.669,
     'L3_gnn_bv2': 2.718,
     'L3_gnn_bs2': 2.848}
    for name, (base, spread) in spreads.items():
        noise = np.random.default_rng([zlib.crc32(name.encode()), seed]).standard_normal(out[name].shape)
        drawn = base * np.exp(spread * noise) if base else spread * noise
        out[name] = jnp.asarray(drawn.astype(out[name].dtype))
    for name, factor in factors.items():
        out[name] = (out[name] * factor).astype(out[name].dtype)
    return out
```

```python
import concourse.bass as bass
from concourse import mybir
from contextlib import ExitStack

NODES = 3125
EDGES = 103125
D = 64
FE = 32
RELS = 8
LN_EPS = 1e-5
NORM_EPS = 1e-12

P = 128
NT = -(-NODES // P)
NPAD = NT * P
LAST = NODES - (NT - 1) * P
G = 4
S = G * P
SLOTS4 = 4
NG = -(-((EDGES + NT * (S - 1)) // S) // SLOTS4) * SLOTS4
NSLOT = NG * S

EP, EC = 125, 825
CB = 11
NSC = 3
NBLK = EC // CB
RC = CB * NSC
RANK_STEPS = 8
assert RC * NT <= EC

R0 = 2
FW = 3 * FE // 2
RF = FW + 5
M_SRC, M_REL, M_LO, M_W, M_A = range(5)
SCRATCH_KIND = "Internal"
XW_ = 130
VAL = D
NV = D + 2

MASKED = 2.0 ** 100
NEW_BUCKET = -2.0 ** 110
NO_BOUND = 2.0 ** 120


def gnn_kernel(nc, x, src, dst, attr, etype, ew, ew1, w1s, w1d, w1e, w2b, wi, wh, xw_w,
               wq, bq, ka, wva, wsa, out, scratch):
    f32, i32, bf16 = mybir.dt.float32, mybir.dt.int32, mybir.dt.bfloat16
    ALU, ACT, AX = mybir.AluOpType, mybir.ActivationFunctionType, mybir.AxisListType
    ds = bass.ds
    t_edge0, t_edge1, t_xn, t_a, t_rel, t_x3, t_h = scratch

    ctx = ExitStack()
    with ctx:
        def sb(name, shape, dt=f32):
            return ctx.enter_context(nc.sbuf_tensor(name, shape, dt))

        def sem(name):
            return ctx.enter_context(nc.semaphore(name))

        iota_i = sb("iota_i", [P, P], i32)
        iota = sb("iota", [P, P])
        part_i = sb("part_i", [P, 1], i32)
        part = sb("part", [P, 1])
        ident = sb("ident", [P, P])
        before = sb("before", [P, P])
        ones = sb("ones", [P, P])
        ident_h = sb("ident_h", [P, P], bf16)
        iota_h = sb("iota_h", [P, P], bf16)
        pick = sb("pick", [2 * G, G, P], bf16)
        pick_at = sb("pick_at", [2 * G, G])
        gnum = sb("gnum", [P, NG])
        vrow_i = sb("vrow_i", [P, NT], i32)
        vrow = sb("vrow", [P, NT])

        w1s_t = sb("w1s_t", [D, D])
        w1d_t = sb("w1d_t", [D + 1, D])
        w1e_t = sb("w1e_t", [3 * FE, D])
        w1e_r = sb("w1e_r", [3 * FE, D])
        w1e_3 = sb("w1e_3", [3 * FE, 3, D], bf16)
        w2b_t = sb("w2b_t", [D + 1, D])
        wi_t = sb("wi_t", [D + 1, 3 * D])
        wh_t = sb("wh_t", [D + 1, 3 * D])
        rel_t = sb("rel_t", [D, RELS * D])
        wq_t = [sb(f"wq_t{i}", [D, D]) for i in range(2)]
        bq_t = [sb(f"bq_t{i}", [D, 1]) for i in range(2)]
        ka_t = [sb(f"ka_t{i}", [D, NV]) for i in range(2)]
        wva_t = [sb(f"wva_t{i}", [NV, D]) for i in range(2)]
        wsa_t = [sb(f"wsa_t{i}", [D + 1, D]) for i in range(2)]

        X = sb("X", [P, NT, D])
        Wk = sb("Wk", [P, NT, D])
        Wk2 = sb("Wk2", [P, NT, D])
        xT = sb("xT", [D + 1, NPAD])
        qT_all = sb("qT_all", [P, NPAD])
        qT = qT_all[0:NV, :]
        mT = sb("mT", [D + 1, NPAD])
        OUT = sb("OUT", [P, NT * NV])
        big = sb("big", [P, NT * 4 * D])
        stat = sb("stat", [P, 4, NT])
        Bt = big[:, 0:NT * D]
        qf = big[:, 0:NT * NV]
        rest = big[:, NT * 2 * D:NT * 2 * D + NT * NV]
        node3 = sb("node3", [P, NT * 3 * NV], bf16)

        sort_a = sb("sort_a", [P, 6 * EC])
        sort_b = sb("sort_b", [P, 7 * EC])

        def part_of(whole, i):
            return whole[0:EP, i * EC:(i + 1) * EC]
        mask, csum, hi_f = (part_of(sort_a, i) for i in range(3))
        part_key_i = part_of(sort_a, 3).bitcast(i32)
        key_i = [part_of(sort_a, 4 + i).bitcast(i32) for i in range(2)]
        key_f = [part_of(sort_b, i) for i in range(2)]
        lo_f = [part_of(sort_b, 2 + i) for i in range(2)]
        rel_f, w_in, a_in = (part_of(sort_b, 4 + i) for i in range(3))
        pos = [sb(f"pos{i}", [EP, EC]) for i in range(2)]
        rel_i = sb("rel_i", [EP, EC], i32)
        cnt = sb("cnt", [EP, NT])
        srt = sb("srt", [P, 6, NT])
        srt_i = sb("srt_i", [P, NT], i32)
        zrow = sb("zrow", [P, NT])
        cmp = big[:, 0:NG * (NT - 1)]
        bucket_f = big[:, NG * (NT - 1):NG * NT]
        cap = [sb(f"cap{i}", [P, NG]) for i in range(2)]
        gnum_i = cap[0].bitcast(i32)
        bucket = [sb(f"bucket{i}", [1, NG], i32) for i in range(2)]
        attr_in = sb("attr_in", [EP, NSC, CB * FE])
        row0 = sb("row0", [EP, NSC, CB * R0])
        row1 = sb("row1", [EP, NSC, CB * RF])
        slot_i = sb("slot_i", [EP, NSC, CB], i32)
        FILL = NSLOT // P // 16
        fill = qT_all[:, 0:FILL * RF]

        meta0 = sb("meta0", [P, NG * G, R0])
        MF = RF - FW
        meta1 = sort_a[:, 0:NG * G * MF].rearrange("p (e f) -> p e f", f=MF)
        gidx = sb("gidx", [P, SLOTS4, G], i32)
        xg = sb("xg", [P, SLOTS4, G, XW_])
        rows = sb("rows", [P, SLOTS4, G * RF])
        OH = sb("OH", [P, SLOTS4, G, P], bf16)

        def of_b(a, n, *shape):
            v = sort_b[:, a:a + n]
            return v.rearrange("p (n s) -> p n s", n=shape[0]) if shape else v
        OHW = of_b(0, SLOTS4 * S, SLOTS4)
        OHT = of_b(2048, SLOTS4 * S // 2, SLOTS4).bitcast(bf16)
        pen = of_b(3072, S, 2).bitcast(bf16)
        sm = of_b(3584, S)
        hsum = of_b(4096, 2 * G * D, 2)
        hres = of_b(4608, 2 * G * D, 2)
        fT = sb("fT", [3 * FE, 2, S], bf16)
        prod = of_b(5120, 2 * G * NV, 2)
        score = sb("score", [P, 2, G])
        score2 = sb("score2", [P, 2, G, 2], bf16)
        scoreT = sb("scoreT", [2 * G, 2, P], bf16)
        less = sb("less", [P, 2, G])
        wgt = sb("wgt", [P, 2, G])
        ref_old = sb("ref_old", [P, 2])
        ref_new = sb("ref_new", [P, 2])
        ref2 = sb("ref2", [P, 2, 2], bf16)
        max_new = sb("max_new", [P, 2])
        fade = sb("fade", [P, SLOTS4])
        faded = sb("faded", [P, 2, NV])
        masked_b = sb("masked_b", [P, 1])
        hid = sb("hid", [P, 2, G, 3, D + 1], bf16)
        gates = big[:, :].rearrange("p (t f) -> p t f", f=4 * D)

        PS = ctx.enter_context(nc.psum_tensor("PS", [P, 8, 512], f32))

        def banks(b, n=1):
            return PS[:, b:b + n, :].rearrange("p b c -> p (b c)")

        def bank_h(b):
            return banks(b).bitcast(bf16)

        s_const = sem("constants_ready")
        s_iota = sem("iotas_written")
        s_wts = sem("weights_loaded")
        s_x = sem("x_loaded")
        s_key = [sem(f"key{i}_loaded") for i in range(2)]
        s_rel = sem("edge_scalars_loaded")
        s_dch = sem("dve_step_done")
        s_cnt = [sem(f"counts{i}_ready") for i in range(2)]
        s_pre = [sem(f"prefixes{i}_ready") for i in range(2)]
        s_rank = sem("rank_step_done")
        s_pos = [sem(f"positions{i}_ready") for i in range(2)]
        s_bkt = [sem(f"buckets{i}_ready") for i in range(2)]
        s_fillt = sem("fill_tile_ready")
        s_fill0 = sem("edge_table0_cleared")
        s_fill1 = sem("edge_table1_cleared")
        s_pack = [sem(f"block{i}_packed") for i in range(2)]
        s_sc = [[sem(f"block{i}_scattered{j}") for j in range(NSC)] for i in range(2)]
        s_at = [sem(f"attr_block_loaded{j}") for j in range(NSC)]
        s_meta = [sem(f"meta{i}_loaded") for i in range(2)]

        class Count:
            def __init__(self, s, base):
                self.sem, self.base = s, base

        ALL = {n: sem(n) for n in ("idx_written", "onehot_written", "group_summed", "sums_added")}
        ATT = {n: sem(n) for n in (
            "attribute_written", "onehot_transposed", "onehot_copied", "penalty_written", "queries_gathered",
            "products_written", "scores_written", "scores_head", "scores_split", "scores_transposed",
            "scores_copied", "scores_spread", "old_reference_read", "new_max_ready", "reference_head",
            "reference_split", "reference_ready", "sums_stored", "reference_gathered",
            "score_less_reference", "weight_ready", "fade_ready", "weighted_onehot")}
        MSG = {n: sem("msg_" + n) for n in (
            "onehot_transposed", "onehot_copied", "features_transposed", "features_copied",
            "hidden_ready", "hidden_added", "head_ready", "rest_ready", "middle_ready", "tail_ready")}
        s_gather = [sem(f"rows_gathered{j}") for j in range(SLOTS4)]
        s_rows = [sem(f"features_loaded{j}") for j in range(SLOTS4)]
        s_table = [sem(f"table{i}_in_dram") for i in range(5)]

        class Pass:
            def __init__(self, i, attention):
                self.i = i
                self.start = s_table[i]
                self.idx = Count(ALL["idx_written"], i * NG)
                self.oh = Count(ALL["onehot_written"], i * NG)
                self.sum = Count(ALL["group_summed"], i * NG)
                self.acc = Count(ALL["sums_added"], i * NG)
                if attention is not None:
                    (self.acol, self.toh, self.ohT, self.pen, self.qg, self.prod, self.score, self.s_hi, self.s2,
                     self.sT, self.sTc, self.spread, self.ro, self.mn, self.r_hi, self.r2, self.rn, self.stored,
                     self.rg, self.less, self.w, self.fade, self.ohw) = (
                        Count(s, attention * NG) for s in ATT.values())
                    if attention:
                        self.acol = Count(ATT["attribute_written"], (attention - 1) * NG)
                    self.K = D if attention == 0 else NV
                    self.key0 = 0 if attention == 0 else VAL
                if i == 1:
                    (self.toh, self.ohT, self.tf, self.fT, self.hidden, self.hsum, self.hi, self.rest,
                     self.mid, self.lo) = (Count(s, 0) for s in MSG.values())
                self.meta = meta0 if i == 0 else meta1
                self.key = 0 if i == 0 else 1
                self.m_idx = (0, M_SRC, M_REL, M_SRC, M_SRC)[i]
                self.m_lo = 1 if i == 0 else M_LO

        passes = [Pass(0, 0), Pass(1, None), Pass(2, None), Pass(3, 1), Pass(4, 2)]

        def pair(name):
            return sem(name + "_on_pe"), sem(name + "_copied")
        s_sq = sem("norm_squares_ready")
        s_nrm = sem("norms_ready")
        s_hn = sem("unit_nodes_ready")
        s_n3 = sem("node_rows_split")
        s_split = sem("features_split")
        s_spc = sem("features_split_step")
        s_var = sem("variances_ready")
        s_std = sem("deviations_ready")
        s_X = sem("nodes_ready")
        s_xT = [pair(f"nodes_transposed{i}") for i in range(3)]
        s_A = pair("message_tables")
        s_aT = pair("sums_transposed")
        s_mT = pair("messages")
        s_gate = pair("gates")
        s_cand = sem("candidate_input_ready")
        s_tanh = sem("candidate_ready")
        s_xw = pair("relation_tables")
        s_xwo = [sem(f"relation_table_stored{i}") for i in range(4)]
        s_q = [pair(f"queries{i}") for i in range(2)]
        s_qk = [pair(f"folded_queries{i}") for i in range(2)]
        s_on = [sem(f"attention_normalised{i}") for i in range(2)]
        s_oT = [pair(f"attention_transposed{i}") for i in range(2)]
        s_y = [pair(f"conv_out{i}") for i in range(2)]
        s_hT = pair("hidden_transposed")
        s_out = sem("output_written")

        class Group:
            def __init__(self, k, c, q):
                self.k, self.ring, self.uses = k, c % SLOTS4, q + c // SLOTS4
                self.par = c % 2
                self.static = isinstance(k, int)

        def sweep(e, step):
            def peeled(t):
                step(lambda off: Group(t + off, (t + off) % SLOTS4, (t + off) // SLOTS4)
                     if 0 <= t + off < NG else None)
            for t in range(-2, SLOTS4):
                peeled(t)
            with e.Fori(1, NG // SLOTS4 - 1) as q:
                for c in range(SLOTS4):
                    step(lambda off: Group(q * SLOTS4 + (c + off), c + off, q))
            for t in range(NG - SLOTS4, NG + 3):
                peeled(t)

        def wait_done(e, count, g, back=0):
            if g.static and count.base == 0 and g.k < back:
                return
            e.wait_ge(count.sem, g.k + (count.base + 1 - back))

        def wait_ring(e, sems, base, g, n):
            e.wait_ge(sems[g.ring], g.uses * (16 * n) + (base // SLOTS4 + 1) * 16 * n)

        def bucket_of(e, q, g):
            return e.value_load(bucket[q.key][0:1, ds(g.k, 1)], min_val=0, max_val=NT - 1)

        def tile(t):
            return slice(t * P, (t + 1) * P)

        def done(s, e):
            e.wait_ge(s.sem, s.base + NG)

        WEIGHTS = [(w1s_t, w1s), (w1d_t, w1d), *((w1e_t[i * FE:(i + 1) * FE, :], w1e) for i in range(3)), (w2b_t, w2b), (wi_t, wi), (wh_t, wh), (rel_t, xw_w)]
        for i in range(2):
            WEIGHTS += [(wq_t[i], wq[i]), (bq_t[i], bq[i]), (ka_t[i], ka[i]), (wva_t[i], wva[i]), (wsa_t[i], wsa[i])]

        block = ctx.enter_context(nc.Block())

        @block.gpsimd
        def _(pool):
            pool.iota(iota_i[:, :], pattern=[[1, P]], base=0, channel_multiplier=0)
            pool.iota(part_i[:, :], pattern=[[0, 1]], base=0, channel_multiplier=1)
            pool.iota(vrow_i[:, :], pattern=[[1, NT]], base=0, channel_multiplier=0)
            pool.iota(gnum_i[:, :], pattern=[[1, NG]], base=0, channel_multiplier=0).then_inc(s_iota, 1)
            pool.memset(fill[:, :], 0.0).then_inc(s_fillt, 1)
            pool.wait_ge(s_fillt, 1)
            pool.memset(fill[:, :].rearrange("p (r f) -> p r f", f=RF)[:, :, FW + M_LO:FW + M_LO + 1], -1.0)\
                .then_inc(s_fillt, 1)
            pool.memset(xg[:, :, :, :], 0.0).then_inc(s_fillt, 1)
            pool.wait_ge(s_fillt, 3)
            pool.memset(xg[:, :, :, XW_ - 1:XW_], 1.0).then_inc(s_fillt, 1)
            pool.memset(meta0[:, :, 0:1], 0.0)
            pool.memset(meta0[:, :, 1:2], -1.0).then_inc(s_fillt, 1)

            for i, (row, width, table, cleared, nfill) in enumerate(
                    ((row0, R0, t_edge0, s_fill0, 1), (row1, RF, t_edge1, s_fill1, 16))):
                pool.wait_ge(cleared, 16 * nfill)

                def scatter(q):
                    for j in range(NSC):
                        if i == 1:
                            pool.wait_ge(s_split, q * NSC + (j + 1))
                        pool.wait_ge(s_pack[i], q * NSC + (j + 1))
                        pool.nop(nofuse=True)
                        for c in range(CB):
                            pool.indirect_dma_start(
                                out=table[:, :], in_=row[:, j, c * width:(c + 1) * width], in_offset=None,
                                out_offset=bass.IndirectOffsetOnAxis(ap=slot_i[:, j, c:c + 1], axis=0))\
                                .then_inc(s_sc[i][j], 16)
                scatter(0)
                with pool.Fori(1, NBLK // NSC) as q:
                    scatter(q)

            for i, (q, table, cols) in enumerate(zip(
                    passes, (t_xn, t_a, t_rel, t_x3, t_h),
                    (slice(0, 2 * D), *[slice(VAL, VAL + D)] * 4))):
                pool.wait_ge(q.start, 16 * (NT if i == 2 else 1))

                def gather(g):
                    wait_done(pool, q.idx, g)
                    pool.nop(nofuse=True)
                    for j in range(G):
                        pool.indirect_dma_start(
                            out=xg[:, g.ring, j, cols], out_offset=None, in_=table[:, :],
                            in_offset=bass.IndirectOffsetOnAxis(ap=gidx[:, g.ring, j:j + 1], axis=0))\
                            .then_inc(s_gather[g.ring], 16)
                sweep(pool, lambda at: at(0) and gather(at(0)))

        @block.sync
        def _(sp):
            for i, k in enumerate((src, dst)):
                sp.dma_start(key_i[i][:, :], k.rearrange("(p c) -> p c", c=EC)).then_inc(s_key[i], 16)
            sp.dma_start(rel_i[:, :], etype.rearrange("(p c) -> p c", c=EC)).then_inc(s_rel, 16)
            sp.dma_start(w_in[:, :], ew.rearrange("(p c) -> p c", c=EC)).then_inc(s_rel, 16)
            sp.dma_start(a_in[:, :], ew1.rearrange("(p c) o -> p (c o)", c=EC)).then_inc(s_rel, 16)
            sp.wait_ge(s_X, 1)
            sp.dma_start(X[:, 0:NT - 1, :], x[0:(NT - 1) * P, :].rearrange("(t p) f -> p t f", p=P)).then_inc(s_x, 16)
            sp.dma_start(X[0:LAST, NT - 1, :], x[(NT - 1) * P:NODES, :]).then_inc(s_x, 16)
            for t, d in WEIGHTS:
                sp.dma_start(t[:, :], d).then_inc(s_wts, 16)
            sp.wait_ge(s_fillt, 5)
            sp.dma_start(t_edge0.rearrange("(p r) f -> p (r f)", p=P),
                         meta0[:, :, :].rearrange("p r f -> p (r f)")).then_inc(s_fill0, 16)
            e1 = t_edge1.rearrange("(p r) f -> p (r f)", p=P)
            for i in range(16):
                sp.dma_start(e1[:, i * FILL * RF:(i + 1) * FILL * RF], fill[:, :]).then_inc(s_fill1, 16)

            at_v = attr.rearrange("(p c) f -> p (c f)", c=EC)

            def load_attr(q):
                for j in range(NSC):
                    if not isinstance(q, int):
                        sp.wait_ge(s_split, q * NSC + (j + 1 - NSC))
                    sp.dma_start(attr_in[:, j, :], at_v[:, ds((q * NSC + j) * (CB * FE), CB * FE)])\
                        .then_inc(s_at[j], 16)
            load_attr(0)
            with sp.Fori(1, NBLK // NSC) as q:
                load_attr(q)

            sp.wait_ge(s_hn, 1)
            sp.dma_start(t_xn.rearrange("(t p) f -> p t f", p=P),
                         big[:, 0:NT * 2 * D].rearrange("p (t f) -> p t f", t=NT)).then_inc(passes[0].start, 16)

            for i, (meta, table, w0, w1) in enumerate(((meta0, t_edge0, 0, R0), (meta1, t_edge1, FW, RF))):
                for j in range(NSC):
                    sp.wait_ge(s_sc[i][j], 16 * EC // NSC)
                tv = table.rearrange("(g p j) f -> p g j f", p=P, j=G)
                H = NG // SLOTS4
                mv = meta[:, :, :].rearrange("p (g j) f -> p g j f", j=G)
                for h in range(SLOTS4):
                    for j in range(G):
                        sp.dma_start(mv[:, h * H:(h + 1) * H, j, :], tv[:, h * H:(h + 1) * H, j, w0:w1])\
                            .then_inc(s_meta[i], 16)

            sp.wait_ge(s_A[1], 5)
            sp.dma_start(t_a.rearrange("(t p) f -> p t f", p=P), Wk[:, :, :]).then_inc(passes[1].start, 16)
            q1 = passes[1]
            rv = t_edge1.rearrange("(g p j) f -> g p (j f)", p=P, j=G)

            def load_rows(g):
                wait_done(sp, q1.tf, g, back=SLOTS4)
                sp.dma_start(rows[:, g.ring, :], rv[ds(g.k, 1), :, :].rearrange("a p f -> p (a f)"))\
                    .then_inc(s_rows[g.ring], 16)
            sweep(sp, lambda at: at(0) and load_rows(at(0)))

            xwv = t_rel.rearrange("(r t p) f -> t p r f", r=RELS, p=P)
            for t in range(NT):
                sp.wait_ge(s_xw[1], t + 1)
                sp.dma_start(xwv[t, :, :, :], big[:, (t % 4) * 512:(t % 4 + 1) * 512]
                             .rearrange("p (r f) -> p r f", r=RELS)).then_inc(s_xwo[t % 4], 16)
            for j in range(4):
                sp.wait_ge(s_xwo[j], 16 * len(range(j, NT, 4)))
            sp.sem_inc(passes[2].start, 16 * NT)

            sp.wait_ge(s_X, 4)
            sp.dma_start(t_x3.rearrange("(t p) f -> p t f", p=P), X[:, :, :]).then_inc(passes[3].start, 16)
            sp.wait_ge(s_y[0][1], 5)
            sp.dma_start(t_h.rearrange("(t p) f -> p t f", p=P), Wk2[:, :, :]).then_inc(passes[4].start, 16)

            sp.wait_ge(s_X, 5)
            sp.dma_start(out[0:(NT - 1) * P, :].rearrange("(t p) f -> p t f", p=P), X[:, 0:NT - 1, :]).then_inc(s_out, 16)
            sp.dma_start(out[(NT - 1) * P:NODES, :], X[0:LAST, NT - 1, :]).then_inc(s_out, 16)
            sp.wait_ge(s_out, 32)

        @block.tensor
        def _(pe):
            mm, tr = nc.tensor.matmul, nc.tensor.transpose
            pe.wait_ge(s_const, 1)
            for i in range(2):
                pe.wait_ge(s_cnt[i], 1)
                mm(banks(7)[:, 0:NT], before[0:EP, :], cnt[:, :], start=True, stop=True)
                mm(banks(7)[:, 32:32 + NT], ones[0:EP, :], cnt[:, :], start=True, stop=True).then_inc(s_pre[i], 1)

            def transposes(source, width, on_pe, copied):
                for b in range(5):
                    if b >= 2:
                        pe.wait_ge(copied, b - 1)
                    for j in range(5):
                        last = tr(banks(2 * (b % 2), 2)[0:width, tile(j)], source(5 * b + j), ident[:, :])
                    last.then_inc(on_pe, 1)

            def project(weight, source, rows, width, on_pe, copied):
                for b in range(5):
                    if b >= 2:
                        pe.wait_ge(copied, b - 1)
                    for c0, c1 in ((0, 512), (512, 5 * P)):
                        last = mm(banks(4 + 2 * (b % 2), 2)[0:width, c0:c1], weight,
                                  source[0:rows, b * 5 * P + c0:b * 5 * P + c1], start=True, stop=True)
                    last.then_inc(on_pe, 1)

            def turn_onehot(q, bank, g):
                wait_done(pe, q.oh, g)
                wait_done(pe, q.ohT, g, back=1)
                for j in range(G):
                    last = tr(bank_h(bank)[:, tile(j)], OH[:, g.ring, j, :], ident_h[:, :])
                last.then_inc(q.toh.sem, 1)

            def attention(q):
                def queries(g, b):
                    wait_done(pe, q.ohT, g)
                    wait_done(pe, q.prod, g, back=1)
                    pe.nop(nofuse=True)
                    for j in range(G):
                        for part_ in range(3):
                            last = mm(banks(0)[:, j * q.K:(j + 1) * q.K], OHT[:, g.ring, tile(j)],
                                      node3[:, ds(b * (3 * q.K) + part_ * q.K, q.K)],
                                      start=(part_ == 0), stop=(part_ == 2))
                    last.then_inc(q.qg.sem, 1)

                def sums(g):
                    wait_done(pe, q.ohw, g)
                    wait_done(pe, q.acc, g, back=2)
                    for j in range(G):
                        last = mm(banks(6 + g.par)[:, 0:NV], OHW[:, g.ring, tile(j)], xg[:, g.ring, j, VAL:XW_],
                                  start=(j == 0), stop=(j == G - 1))
                    last.then_inc(q.sum.sem, 1)

                def references(g):
                    wait_done(pe, q.r2, g)
                    wait_done(pe, q.less, g, back=1)
                    for j in range(G):
                        for part_ in range(2):
                            last = mm(banks(3)[:, j:j + 1], OHT[:, g.ring, tile(j)], ref2[:, g.par, part_:part_ + 1],
                                      start=(part_ == 0), stop=(part_ == 1))
                    last.then_inc(q.rg.sem, 1)

                def turn_scores(g):
                    wait_done(pe, q.s2, g)
                    wait_done(pe, q.sTc, g, back=1)
                    tr(bank_h(2)[0:2 * G, 0:P], score2[:, g.par, :, :].rearrange("p j h -> p (j h)"),
                       ident_h[:, :]).then_inc(q.sT.sem, 1)

                def spread(g):
                    wait_done(pe, q.sTc, g)
                    wait_done(pe, q.mn, g, back=2)
                    for j in range(G):
                        last = mm(banks(4 + g.par)[:, tile(j)], pick[:, j, :], scoreT[:, g.par, :],
                                  start=True, stop=True)
                    last.then_inc(q.spread.sem, 1)

                def step(at):
                    b = bucket_of(pe, q, at(1)) if at(1) else None
                    if at(-2):
                        sums(at(-2))
                    if at(-1):
                        references(at(-1))
                    if at(0):
                        turn_scores(at(0))
                    if at(1):
                        queries(at(1), b)
                    if at(0):
                        spread(at(0))
                    if at(2):
                        turn_onehot(q, 1, at(2))
                sweep(pe, step)

            pe.wait_ge(s_n3, 1)
            attention(passes[0])

            pe.wait_ge(s_X, 2)
            pe.wait_ge(s_wts, 16 * len(WEIGHTS))
            transposes(lambda t: X[:, t, :], D, *s_xT[0])
            pe.wait_ge(s_xT[0][1], 5)
            for b in range(10):
                if b >= 4:
                    pe.wait_ge(s_A[1], b - 3)
                rows_in, w = (D, w1s_t) if b < 5 else (D + 1, w1d_t)
                for j in range(5):
                    last = mm(banks(4 + b % 4)[:, j * D:(j + 1) * D], xT[0:rows_in, tile(5 * (b % 5) + j)], w[:, :],
                              start=True, stop=True)
                last.then_inc(s_A[0], 1)
            pe.wait_ge(s_A[1], 10)
            pe.wait_ge(s_n3, 2)
            q = passes[1]

            def turn_features(g):
                wait_ring(pe, s_rows, 0, g, 1)
                wait_done(pe, q.fT, g, back=1)
                for j in range(G):
                    last = tr(bank_h(0)[0:3 * FE, tile(j)],
                              rows[:, g.ring, j * RF:j * RF + FW].bitcast(bf16), ident_h[:, :])
                last.then_inc(q.tf.sem, 1)

            def hidden(g):
                b = bucket_of(pe, q, g)
                wait_done(pe, q.ohT, g)
                wait_done(pe, q.fT, g)
                wait_done(pe, q.hsum, g, back=2)
                pe.nop(nofuse=True)
                for j in range(G):
                    o = banks(2 + g.par)[:, j * D:(j + 1) * D]
                    for part_ in range(3):
                        mm(o, OHT[:, g.ring, tile(j)], node3[:, ds(b * (3 * D) + part_ * D, D)],
                           start=(part_ == 0), stop=False)
                    for part_ in range(3):
                        last = mm(o, fT[:, g.par, tile(j)], w1e_3[:, part_, :], start=False, stop=(part_ == 2))
                last.then_inc(q.hidden.sem, 1)

            def message_sums(g):
                wait_done(pe, q.lo, g)
                wait_done(pe, q.acc, g, back=2)
                for j in range(G):
                    for part_ in range(3):
                        last = mm(banks(6 + g.par)[:, 0:D + 1], OH[:, g.ring, j, :], hid[:, g.par, j, part_, :],
                                  start=(j + part_ == 0), stop=(j == G - 1 and part_ == 2))
                last.then_inc(q.sum.sem, 1)

            def step(at):
                if at(0):
                    hidden(at(0))
                if at(1):
                    turn_onehot(q, 1, at(1))
                    turn_features(at(1))
                if at(-1):
                    message_sums(at(-1))
            sweep(pe, step)

            done(q.acc, pe)
            transposes(lambda t: OUT[:, t * NV:t * NV + D + 1], D + 1, *s_aT)
            pe.wait_ge(s_aT[1], 5)
            project(w2b_t[:, :], qT, D + 1, D, *s_mT)
            pe.wait_ge(s_mT[1], 5)
            for b in range(5):
                if b >= 2:
                    pe.wait_ge(s_gate[1], 2 * (b - 1))
                for j in range(5):
                    o = banks(3 * (b % 2), 3)[:, j * 4 * D:(j + 1) * 4 * D]
                    mm(o[:, 0:3 * D], mT[:, tile(5 * b + j)], wi_t[:, :], start=True, stop=False, skip_group_check=True)
                    mm(o[:, 0:2 * D], xT[:, tile(5 * b + j)], wh_t[:, 0:2 * D], start=False, stop=True, skip_group_check=True)
                    last = mm(o[:, 3 * D:4 * D], xT[:, tile(5 * b + j)], wh_t[:, 2 * D:3 * D], start=True, stop=True, skip_group_check=True)
                last.then_inc(s_gate[0], 1)

            pe.wait_ge(s_X, 3)
            transposes(lambda t: X[:, t, :], D, *s_xT[1])
            pe.wait_ge(s_xT[1][1], 5)
            for t in range(NT):
                if t >= 4:
                    pe.wait_ge(s_xw[1], t - 3)
                mm(banks(4 + t % 4), xT[0:D, tile(t)], rel_t[:, :], start=True, stop=True).then_inc(s_xw[0], 1)
            pe.wait_ge(s_xw[1], NT)
            q = passes[2]

            def relation_sums(g):
                wait_ring(pe, s_gather, 2 * NG, g, G)
                wait_done(pe, q.oh, g)
                wait_done(pe, q.acc, g, back=2)
                for j in range(G):
                    last = mm(banks(6 + g.par)[:, 0:D], OHW[:, g.ring, tile(j)], xg[:, g.ring, j, VAL:VAL + D],
                              start=(j == 0), stop=(j == G - 1))
                last.then_inc(q.sum.sem, 1)
            sweep(pe, lambda at: at(0) and relation_sums(at(0)))

            for i in range(2):
                if i == 0:
                    pe.wait_ge(s_X, 4)
                    transposes(lambda t: X[:, t, :], D, *s_xT[2])
                    pe.wait_ge(s_xT[2][1], 5)
                else:
                    pe.wait_ge(s_y[0][1], 5)
                    transposes(lambda t: Wk2[:, t, :], D, *s_hT)
                    pe.wait_ge(s_hT[1], 5)
                project(wq_t[i][:, :], xT, D, D, *s_q[i])
                pe.wait_ge(s_q[i][1], 5)
                for b in range(5):
                    if b >= 2:
                        pe.wait_ge(s_qk[i][1], b - 1)
                    for j in range(5):
                        last = mm(banks(2 + b % 2)[:, j * NV:(j + 1) * NV], mT[0:D, tile(5 * b + j)], ka_t[i][:, :],
                                  start=True, stop=True)
                    last.then_inc(s_qk[i][0], 1)
                pe.wait_ge(s_n3, 3 + i)
                attention(passes[3 + i])
                pe.wait_ge(s_on[i], 1)
                transposes(lambda t: OUT[:, t * NV:(t + 1) * NV], NV, *s_oT[i])
                pe.wait_ge(s_oT[i][1], 5)
                for b in range(5):
                    if b >= 2:
                        pe.wait_ge(s_y[i][1], b - 1)
                    for j in range(5):
                        o = banks(4 + b % 2)[:, j * D:(j + 1) * D]
                        mm(o, qT[:, tile(5 * b + j)], wva_t[i][:, :], start=True, stop=False)
                        last = mm(o, xT[:, tile(5 * b + j)], wsa_t[i][:, :], start=False, stop=True)
                    last.then_inc(s_y[i][0], 1)

        @block.scalar
        def _(act):
            A = nc.scalar.activation

            for i in range(2):
                if i == 1:
                    act.wait_ge(s_sq, 1)
                    A(stat[:, 1, :], stat[:, 0, :], ACT.Sqrt).then_inc(s_nrm, 1)
                    for j in range(NSC):
                        act.wait_ge(s_sc[0][j], 16 * EC // NSC)

                def pack(q):
                    for j in range(NSC):
                        if not isinstance(q, int):
                            act.wait_ge(s_sc[i][j], q * (16 * CB))
                            act.nop(nofuse=True)
                        if j == 0:
                            act.wait_ge(s_pos[i], q + 1)
                            act.nop(nofuse=True)
                        c = ds((q * NSC + j) * CB, CB)
                        if i == 0:
                            r = row0[:, j, :].rearrange("p (c f) -> p c f", f=R0)
                            A(r[:, :, 0:1], key_f[1][:, c].unsqueeze(2), ACT.Copy)
                            A(r[:, :, 1:2], lo_f[0][:, c].unsqueeze(2), ACT.Copy)
                        else:
                            r = row1[:, j, :].rearrange("p (c f) -> p c f", f=RF)
                            for m, src_ in ((M_SRC, key_f[0]), (M_REL, rel_f), (M_LO, lo_f[1]), (M_W, w_in), (M_A, a_in)):
                                A(r[:, :, FW + m:FW + m + 1], src_[:, c].unsqueeze(2), ACT.Copy)
                        A(slot_i[:, j, :], pos[i][:, c], ACT.Copy).then_inc(s_pack[i], 1)
                pack(0)
                with act.Fori(1, NBLK // NSC) as q:
                    pack(q)

            def copy_pairs(dst_, width, on_pe, copied, func=ACT.Copy, first=4, **kw):
                for b in range(5):
                    act.wait_ge(on_pe, b + 1)
                    A(dst_[0:width, b * 5 * P:(b + 1) * 5 * P], banks(first + 2 * (b % 2), 2)[0:width, 0:5 * P],
                      func, **kw).then_inc(copied, 1)

            def prepare_first(q):
                act.wait_ge(s_meta[q.key], 16 * SLOTS4 * G)
                for k in range(SLOTS4):
                    prepare(q, Group(k, k, 0))

            def prepare_next(q, g):
                if g and not (g.static and g.k < SLOTS4):
                    prepare(q, g)

            def prepare(q, g):
                wait_done(act, q.sum, g, back=SLOTS4)
                act.nop(nofuse=True)
                A(gidx[:, g.ring, :], q.meta[:, ds(g.k * G, G), q.m_idx], ACT.Copy).then_inc(q.idx.sem, 1)
                if q.i >= 3:
                    A(xg[:, g.ring, :, VAL + D], q.meta[:, ds(g.k * G, G), M_A], ACT.Copy).then_inc(q.acol.sem, 1)

            def copy_onehot(q, g):
                wait_done(act, q.toh, g)
                if q.i == 1:
                    wait_done(act, q.sum, g, back=SLOTS4)
                else:
                    wait_done(act, q.rg, g, back=SLOTS4)
                    wait_done(act, q.pen, g, back=SLOTS4)
                A(OHT[:, g.ring, :], bank_h(1)[:, 0:S], ACT.Copy).then_inc(q.ohT.sem, 1)

            def attention(q):
                def penalty(g):
                    wait_done(act, q.ohT, g)
                    wait_done(act, q.mn, g, back=2)
                    A(pen[:, g.par, :], OHT[:, g.ring, :], ACT.Identity, scale=MASKED, bias=masked_b[:, 0:1])\
                        .then_inc(q.pen.sem, 1)

                def fades(g):
                    wait_done(act, q.rn, g)
                    wait_done(act, q.acc, g, back=SLOTS4)
                    A(fade[:, g.ring:g.ring + 1], ref_new[:, g.par:g.par + 1], ACT.Exp, scale=-1.0,
                      bias=ref_old[:, g.par:g.par + 1]).then_inc(q.fade.sem, 1)

                def copy_scores(g):
                    wait_done(act, q.sT, g)
                    wait_done(act, q.spread, g, back=2)
                    A(scoreT[:, g.par, :], bank_h(2)[0:2 * G, 0:P], ACT.Copy).then_inc(q.sTc.sem, 1)

                def weights(g):
                    wait_done(act, q.less, g)
                    wait_done(act, q.ohw, g, back=2)
                    A(wgt[:, g.par, :], less[:, g.par, :], ACT.Exp).then_inc(q.w.sem, 1)

                def store(g):
                    b = bucket_of(act, q, g)
                    wait_done(act, q.acc, g)
                    wait_done(act, q.stored, g, back=1)
                    act.nop(nofuse=True)
                    A(OUT[:, ds(b * NV, NV)], faded[:, g.par, :], ACT.Copy).then_inc(q.stored.sem, 1)

                def step(at):
                    prepare_next(q, at(2))
                    if at(0):
                        copy_scores(at(0))
                    if at(-1):
                        weights(at(-1))
                        fades(at(-1))
                    if at(-3):
                        store(at(-3))
                    if at(1):
                        penalty(at(1))
                    if at(2):
                        copy_onehot(q, at(2))
                sweep(act, step)

            def deviations():
                act.wait_ge(s_var, deviations.n)
                A(stat[:, 3, :], stat[:, 2, :], ACT.Sqrt).then_inc(s_std, 1)
                deviations.n += 1
            deviations.n = 1

            act.wait_ge(s_bkt[0], 1)
            act.wait_ge(s_pack[1], NBLK)
            prepare_first(passes[0])
            attention(passes[0])
            deviations()

            prepare_first(passes[1])
            copy_pairs(xT, D, *s_xT[0], first=0)
            for b in range(10):
                act.wait_ge(s_A[0], b + 1)
                source = banks(4 + b % 4)[:, 0:5 * D]
                if b < 5:
                    A(Wk[:, 5 * b:5 * b + 5, :], source.rearrange("p (t f) -> p t f", f=D), ACT.Copy).then_inc(s_A[1], 1)
                else:
                    A(Bt[:, 5 * (b - 5) * D:5 * (b - 4) * D], source, ACT.Copy).then_inc(s_A[1], 1)
            q = passes[1]

            def copy_features(g):
                wait_done(act, q.tf, g)
                wait_done(act, q.hidden, g, back=2)
                A(fT[:, g.par, :], bank_h(0)[0:3 * FE, 0:S], ACT.Copy).then_inc(q.fT.sem, 1)

            def rows_of(t, g):
                return t[:, g.par, :].rearrange("p (j f) -> p j f", f=D)

            def head(g):
                wait_done(act, q.hsum, g)
                wait_done(act, q.sum, g, back=2)
                A(hid[:, g.par, :, 0, 0:D], rows_of(hsum, g), ACT.Relu).then_inc(q.hi.sem, 1)

            def middle(g):
                wait_done(act, q.rest, g)
                A(hid[:, g.par, :, 1, 0:D], rows_of(hres, g), ACT.Copy).then_inc(q.mid.sem, 1)

            def step(at):
                prepare_next(q, at(2))
                if at(0):
                    head(at(0))
                if at(1):
                    copy_onehot(q, at(1))
                if at(0):
                    middle(at(0))
                if at(1):
                    copy_features(at(1))
            sweep(act, step)
            prepare_first(passes[2])
            copy_pairs(qT, D + 1, *s_aT, first=0)
            copy_pairs(mT, D, *s_mT)
            for b in range(5):
                act.wait_ge(s_gate[0], b + 1)
                g4 = banks(3 * (b % 2), 3)[:, 0:5 * 4 * D].rearrange("p (t f) -> p t f", f=4 * D)
                A(gates[:, 5 * b:5 * b + 5, 0:2 * D], g4[:, :, 0:2 * D], ACT.Sigmoid).then_inc(s_gate[1], 1)
                A(gates[:, 5 * b:5 * b + 5, 2 * D:4 * D], g4[:, :, 2 * D:4 * D], ACT.Copy).then_inc(s_gate[1], 1)
            act.wait_ge(s_cand, 1)
            A(Wk2[:, :, :], Wk[:, :, :], ACT.Tanh).then_inc(s_tanh, 1)
            deviations()

            copy_pairs(xT, D, *s_xT[1], first=0)
            for t in range(NT):
                act.wait_ge(s_xw[0], t + 1)
                if t >= 4:
                    act.wait_ge(s_xwo[t % 4], 16 * (t // 4))
                A(big[:, (t % 4) * 512:(t % 4 + 1) * 512], banks(4 + t % 4), ACT.Copy).then_inc(s_xw[1], 1)
            sweep(act, lambda at: prepare_next(passes[2], at(2)))
            prepare_first(passes[3])
            deviations()

            for i in range(2):
                copy_pairs(xT, D, *(s_xT[2] if i == 0 else s_hT), first=0)
                copy_pairs(mT, D, *s_q[i], func=ACT.Identity, bias=bq_t[i][:, 0:1])
                for b in range(5):
                    act.wait_ge(s_qk[i][0], b + 1)
                    A(qf[:, 5 * b * NV:5 * (b + 1) * NV], banks(2 + b % 2)[:, 0:5 * NV], ACT.Copy,
                      scale=float(D) ** -0.5).then_inc(s_qk[i][1], 1)
                attention(passes[3 + i])
                if i == 0:
                    prepare_first(passes[4])
                copy_pairs(qT, NV, *s_oT[i], first=0)
                for b in range(5):
                    act.wait_ge(s_y[i][0], b + 1)
                    A(Wk2[:, 5 * b:5 * b + 5, :], banks(4 + b % 2)[:, 0:5 * D].rearrange("p (t f) -> p t f", f=D),
                      ACT.Relu if i == 0 else ACT.Copy).then_inc(s_y[i][1], 1)
            deviations()

        @block.vector
        def _(dve):
            V = nc.vector
            steps = [0]

            def link(instruction):
                steps[0] += 1
                instruction.then_inc(s_dch, 1)
                dve.wait_ge(s_dch, steps[0])

            outv = OUT[:, :].rearrange("p (t f) -> p t f", f=NV)

            dve.wait_ge(s_iota, 1)
            V.tensor_copy(iota[:, :], iota_i[:, :])
            V.tensor_copy(part[:, :], part_i[:, :])
            V.tensor_copy(gnum[:, :], gnum_i[:, :])
            V.memset(X[:, NT - 1, :], 0.0).then_inc(s_X, 1)
            V.memset(ones[:, :], 1.0)
            V.memset(zrow[:, :], 0.0)
            V.memset(masked_b[:, :], -MASKED)
            V.memset(hid[:, :, :, :, D:D + 1], 0.0)
            V.tensor_copy(iota_h[:, :], iota_i[:, :])
            link(V.tensor_copy(vrow[:, :], vrow_i[:, :]))
            V.memset(hid[:, :, :, 0, D:D + 1], 1.0)
            V.tensor_scalar(before[:, :], iota[:, :], part[:, 0:1], None, ALU.is_gt)
            V.tensor_scalar(ident_h[:, :], iota[:, :], part[:, 0:1], None, ALU.is_equal)
            link(V.tensor_scalar(pick_at[:, :], iota[0:2 * G, 0:G], -2.0, part[0:2 * G, 0:1], ALU.mult, ALU.add))
            link(V.tensor_scalar(pick_at[:, :], pick_at[:, :], -0.5, None, ALU.add))
            link(V.tensor_tensor(pick_at[:, :], pick_at[:, :], pick_at[:, :], ALU.mult))
            V.tensor_scalar(pick[:, :, :], pick_at[:, :].unsqueeze(2).broadcast_to([2 * G, G, P]), 1.0, None, ALU.is_lt)
            V.tensor_scalar(ident[:, :], iota[:, :], part[:, 0:1], None, ALU.is_equal).then_inc(s_const, 1)

            def split(i):
                dve.wait_ge(s_key[i], 16)
                link(V.tensor_scalar(part_key_i[:, :], key_i[i][:, :], P - 1, None, ALU.bitwise_and))
                V.tensor_copy(key_f[i][:, :], key_i[i][:, :])
                link(V.tensor_copy(lo_f[i][:, :], part_key_i[:, :]))

            mask3, csum3 = (t.rearrange("p (v c) -> p v c", c=RC) for t in (mask, csum))

            def slots(i, q):
                cols = ds(q * RC, RC) if not isinstance(q, int) else slice(q * RC, (q + 1) * RC)
                next_slot, first = srt[0:EP, 4, :], srt[0:EP, 5, :]
                n = q * RANK_STEPS + i * (EC // RC * RANK_STEPS)

                def written(instruction, k):
                    instruction.then_inc(s_rank, 1)
                    dve.wait_ge(s_rank, n + k)
                    dve.nop(nofuse=True)
                written(V.tensor_tensor(mask3, hi_f[:, cols].unsqueeze(1).broadcast_to([EP, NT, RC]),
                                        vrow[0:EP, :].unsqueeze(2).broadcast_to([EP, NT, RC]), ALU.is_equal), 1)
                written(V.tensor_tensor_scan(csum[:, :], mask[:, :], zrow[0:EP, 0:1].broadcast_to([EP, EC]), 0.0,
                                             ALU.add, ALU.max), 2)
                V.tensor_copy(first[:, 0:1], next_slot[:, 0:1]).then_inc(s_rank, 1)
                written(V.tensor_tensor(first[:, 1:NT], next_slot[:, 1:NT], csum3[:, 0:NT - 1, RC - 1], ALU.subtract), 4)
                V.tensor_tensor(next_slot, first, csum3[:, :, RC - 1], ALU.add).then_inc(s_rank, 1)
                dve.wait_ge(s_rank, n + 5)
                dve.nop(nofuse=True)
                written(V.tensor_tensor(csum3, csum3, first.unsqueeze(2).broadcast_to([EP, NT, RC]), ALU.add), 6)
                written(V.tensor_tensor(csum3, csum3, mask3, ALU.mult), 7)
                V.tensor_reduce(pos[i][:, cols], csum3.rearrange("p v c -> p c v"), AX.X, ALU.add).then_inc(s_rank, 1)
                dve.wait_ge(s_rank, n + RANK_STEPS)
                dve.sem_inc(s_pos[i], 1)

            def rank(i):
                link(V.tensor_scalar(part_key_i[:, :], key_i[i][:, :], P.bit_length() - 1, None, ALU.arith_shift_right))
                link(V.tensor_copy(hi_f[:, :], part_key_i[:, :]))
                for v in range(NT):
                    link(V.tensor_scalar(mask[:, :], hi_f[:, :], float(v), None, ALU.is_equal, ALU.add,
                                         accum_out=cnt[:, v:v + 1]))
                dve.sem_inc(s_cnt[i], 1)
                dve.wait_ge(s_pre[i], 1)
                link(V.tensor_scalar(srt[:, 0, :], banks(7)[:, 32:32 + NT], float(S - 1), None, ALU.add))
                link(V.tensor_copy(srt_i[:, :], srt[:, 0, :]))
                link(V.tensor_scalar(srt_i[:, :], srt_i[:, :], S.bit_length() - 1, None, ALU.arith_shift_right))
                link(V.tensor_copy(srt[:, 1, :], srt_i[:, :]))
                link(V.tensor_tensor_scan(srt[:, 2, :], srt[:, 1, :], zrow[:, :], 0.0, ALU.add, ALU.max))
                link(V.tensor_tensor(srt[:, 3, :], srt[:, 2, :], srt[:, 1, :], ALU.subtract))
                link(V.scalar_tensor_tensor(srt[:, 4, :], srt[:, 3, :], float(S), banks(7)[:, 0:NT], ALU.mult, ALU.add))
                link(V.tensor_scalar(srt[:, 4, :], srt[:, 4, :], -1.0, None, ALU.add))
                slots(i, 0)
                with dve.Fori(1, EC // RC) as q:
                    slots(i, q)
                c3 = cmp.rearrange("p (g v) -> p g v", v=NT - 1)
                link(V.tensor_tensor(c3, srt[:, 3, 1:NT].unsqueeze(1).broadcast_to([P, NG, NT - 1]),
                                     gnum[:, :].unsqueeze(2).broadcast_to([P, NG, NT - 1]), ALU.is_le))
                link(V.tensor_reduce(bucket_f, c3, AX.X, ALU.add))
                V.tensor_copy(bucket[i][:, :], bucket_f[0:1, :]).then_inc(s_bkt[i], 1)
                V.memset(cap[i][:, 0:1], 0.0)
                link(V.tensor_tensor(cap[i][:, 1:NG], bucket_f[:, 1:NG], bucket_f[:, 0:NG - 1], ALU.is_equal))
                link(V.tensor_scalar(cap[i][:, 1:NG], cap[i][:, 1:NG], NO_BOUND, None, ALU.mult))
                link(V.tensor_scalar(cap[i][:, :], cap[i][:, :], NEW_BUCKET, None, ALU.add))

            def per_node(column):
                return column.unsqueeze(2).broadcast_to([P, NT, D])

            def layer_norm():
                link(V.tensor_reduce(stat[:, 0, :], Wk[:, :, :], AX.X, ALU.add))
                link(V.tensor_scalar(stat[:, 0, :], stat[:, 0, :], 1.0 / D, None, ALU.mult))
                link(V.tensor_tensor(Wk[:, :, :], Wk[:, :, :], per_node(stat[:, 0, :]), ALU.subtract))
                link(V.tensor_tensor(Wk2[:, :, :], Wk[:, :, :], Wk[:, :, :], ALU.mult))
                link(V.tensor_reduce(stat[:, 1, :], Wk2[:, :, :], AX.X, ALU.add))
                V.tensor_scalar(stat[:, 2, :], stat[:, 1, :], 1.0 / D, LN_EPS, ALU.mult, ALU.add).then_inc(s_var, 1)
                layer_norm.n += 1
                dve.wait_ge(s_std, layer_norm.n)
                link(V.reciprocal(stat[:, 0, :], stat[:, 3, :]))
                link(V.tensor_tensor(X[:, :, :], Wk[:, :, :], per_node(stat[:, 0, :]), ALU.mult))
                dve.sem_inc(s_X, 1)
            layer_norm.n = 0

            def split_nodes(rows_, width):
                r = rows_.rearrange("p (t f) -> p t f", t=NT) if len(rows_.shape) == 2 else rows_
                n3 = node3[:, 0:NT * 3 * width].rearrange("p (t h f) -> p t h f", h=3, f=width)
                left = rest[:, 0:NT * width].rearrange("p (t f) -> p t f", t=NT)
                link(V.tensor_copy(n3[:, :, 0, :], r))
                link(V.tensor_tensor(left, r, n3[:, :, 0, :], ALU.subtract))
                link(V.tensor_copy(n3[:, :, 1, :], left))
                V.tensor_tensor(n3[:, :, 2, :], left, n3[:, :, 1, :], ALU.subtract).then_inc(s_n3, 1)

            def clear(q, attention):
                if attention:
                    V.memset(ref_new[:, :], 0.0)
                    V.memset(faded[:, :, :], 0.0)
                link(V.memset(OUT[:, :], 0.0))

            def onehot(q, g):
                wait_done(dve, q.sum if q.i == 1 else q.ohw, g, back=SLOTS4)
                V.tensor_tensor(OH[:, g.ring, :, :], iota_h[:, :].unsqueeze(1).broadcast_to([P, G, P]),
                                q.meta[:, ds(g.k * G, G), q.m_lo].unsqueeze(2).broadcast_to([P, G, P]),
                                ALU.is_equal).then_inc(q.oh.sem, 1)

            def add_sums(q, g, width):
                b = bucket_of(dve, q, g)
                wait_done(dve, q.sum, g)
                wait_done(dve, q.acc, g, back=1)
                o = OUT[:, ds(b * NV, width)]
                V.tensor_tensor(o, o, banks(6 + g.par)[:, 0:width], ALU.add).then_inc(q.acc.sem, 1)

            def attention(q):
                def add_faded(g):
                    wait_done(dve, q.sum, g)
                    wait_done(dve, q.fade, g)
                    wait_done(dve, q.acc, g, back=1)
                    wait_done(dve, q.stored, g, back=2)
                    V.scalar_tensor_tensor(faded[:, g.par, :], faded[:, 1 - g.par, :], fade[:, g.ring:g.ring + 1],
                                           banks(6 + g.par)[:, 0:NV], ALU.mult, ALU.add).then_inc(q.acc.sem, 1)

                def maxima(g):
                    pm = slice(g.par, g.par + 1)
                    wait_done(dve, q.ro, g)
                    wait_done(dve, q.spread, g)
                    wait_done(dve, q.pen, g)
                    wait_done(dve, q.mn, g, back=1)
                    dve.nop(nofuse=True)
                    V.tensor_tensor_reduce(out=sm, in0=banks(4 + g.par), in1=pen[:, g.par, :],
                                           scale=1.0, scalar=ref_old[:, pm], op0=ALU.add, op1=ALU.max,
                                           accum_out=max_new[:, pm]).then_inc(q.mn.sem, 1)

                def products(g):
                    wait_ring(dve, s_gather, q.i * NG, g, G)
                    if q.i:
                        wait_done(dve, q.acol, g)
                    wait_done(dve, q.qg, g)
                    wait_done(dve, q.score, g, back=2)
                    V.tensor_tensor(prod[:, g.par, 0:G * q.K].rearrange("p (j f) -> p j f", j=G),
                                    banks(0)[:, 0:G * q.K].rearrange("p (j f) -> p j f", j=G),
                                    xg[:, g.ring, :, q.key0:q.key0 + q.K], ALU.mult).then_inc(q.prod.sem, 1)

                def ref_head(g):
                    wait_done(dve, q.mn, g)
                    wait_done(dve, q.rg, g, back=2)
                    wait_done(dve, q.rn, g, back=2)
                    V.tensor_copy(ref2[:, g.par, 0:1], max_new[:, g.par:g.par + 1]).then_inc(q.r_hi.sem, 1)

                def scores(g):
                    wait_done(dve, q.prod, g)
                    wait_done(dve, q.less, g, back=2)
                    V.tensor_reduce(score[:, g.par, :], prod[:, g.par, 0:G * q.K].rearrange("p (j f) -> p j f", j=G),
                                    AX.X, ALU.add).then_inc(q.score.sem, 1)

                def ref_tail(g):
                    wait_done(dve, q.r_hi, g)
                    V.tensor_tensor(ref2[:, g.par, 1:2], max_new[:, g.par:g.par + 1], ref2[:, g.par, 0:1],
                                    ALU.subtract).then_inc(q.r2.sem, 1)

                def score_head(g):
                    wait_done(dve, q.score, g)
                    wait_done(dve, q.sT, g, back=2)
                    V.tensor_copy(score2[:, g.par, :, 0], score[:, g.par, :]).then_inc(q.s_hi.sem, 1)

                def reference(g):
                    wait_done(dve, q.r2, g)
                    wait_done(dve, q.fade, g, back=2)
                    wait_done(dve, q.ro, g, back=1)
                    V.tensor_tensor(ref_new[:, g.par:g.par + 1], ref2[:, g.par, 0:1], ref2[:, g.par, 1:2],
                                    ALU.add).then_inc(q.rn.sem, 1)

                def score_tail(g):
                    wait_done(dve, q.s_hi, g)
                    V.tensor_tensor(score2[:, g.par, :, 1], score[:, g.par, :], score2[:, g.par, :, 0],
                                    ALU.subtract).then_inc(q.s2.sem, 1)

                def old_reference(g):
                    wait_done(dve, q.rn, g, back=1)
                    wait_done(dve, q.fade, g, back=2)
                    dve.nop(nofuse=True)
                    V.tensor_scalar(ref_old[:, g.par:g.par + 1], ref_new[:, 1 - g.par:2 - g.par],
                                    cap[q.key][:, ds(g.k, 1)], None, ALU.min).then_inc(q.ro.sem, 1)

                def subtract_reference(g):
                    wait_done(dve, q.rg, g)
                    wait_done(dve, q.w, g, back=2)
                    V.tensor_tensor(less[:, g.par, :], score[:, g.par, :], banks(3)[:, 0:G], ALU.subtract)\
                        .then_inc(q.less.sem, 1)

                def weighted_onehot(g):
                    wait_done(dve, q.w, g)
                    wait_done(dve, q.sum, g, back=SLOTS4)
                    V.tensor_tensor(OHW[:, g.ring, :].rearrange("p (j n) -> p j n", j=G), OH[:, g.ring, :, :],
                                    wgt[:, g.par, :].unsqueeze(2).broadcast_to([P, G, P]), ALU.mult)\
                        .then_inc(q.ohw.sem, 1)

                def step(at):
                    if at(-1):
                        maxima(at(-1))
                    if at(0):
                        products(at(0))
                    if at(-1):
                        ref_head(at(-1))
                    if at(0):
                        scores(at(0))
                    if at(-1):
                        ref_tail(at(-1))
                    if at(0):
                        score_head(at(0))
                    if at(-1):
                        reference(at(-1))
                    if at(0):
                        score_tail(at(0))
                    if at(0):
                        old_reference(at(0))
                    if at(-1):
                        subtract_reference(at(-1))
                    if at(-3):
                        add_faded(at(-3))
                    if at(2):
                        onehot(q, at(2))
                    if at(-1):
                        weighted_onehot(at(-1))
                sweep(dve, step)
                done(q.stored, dve)
                link(V.tensor_scalar(stat[:, 0, :], outv[:, :, NV - 1], 1e-30, None, ALU.max))
                link(V.reciprocal(stat[:, 1, :], stat[:, 0, :]))

            split(1)
            split(0)
            rank(0)
            V.memset(xT[D:D + 1, :], 1.0)
            V.memset(mT[D:D + 1, :], 1.0)
            dve.wait_ge(s_x, 32)
            link(V.tensor_tensor(Wk[:, :, :], X[:, :, :], X[:, :, :], ALU.mult))
            V.tensor_reduce(stat[:, 0, :], Wk[:, :, :], AX.X, ALU.add).then_inc(s_sq, 1)
            dve.wait_ge(s_rel, 48)
            link(V.tensor_copy(rel_f[:, :], rel_i[:, :]))
            link(V.scalar_tensor_tensor(rel_f[:, :], rel_f[:, :], float(NPAD), key_f[0][:, :], ALU.mult, ALU.add))
            rank(1)

            dve.wait_ge(s_nrm, 1)
            link(V.tensor_scalar(stat[:, 2, :], stat[:, 1, :], NORM_EPS, None, ALU.max))
            link(V.reciprocal(stat[:, 0, :], stat[:, 2, :]))
            xn = big[:, 0:NT * 2 * D].rearrange("p (t f) -> p t f", f=2 * D)
            V.tensor_tensor(xn[:, :, 0:D], X[:, :, :], per_node(stat[:, 0, :]), ALU.mult)
            link(V.tensor_copy(xn[:, :, D:2 * D], X[:, :, :]))
            dve.sem_inc(s_hn, 1)
            split_nodes(xn[:, :, 0:D], D)

            def split_features(q):
                for j in range(NSC):
                    dve.wait_ge(s_at[j], q * 16 + 16)
                    if not isinstance(q, int):
                        dve.wait_ge(s_sc[1][j], q * (16 * CB))
                        dve.nop(nofuse=True)
                    a = attr_in[:, j, :].rearrange("p (c f) -> p c f", f=FE)
                    r = row1[:, j, :].bitcast(bf16).rearrange("p (c f) -> p c f", f=2 * RF)
                    n = (q * NSC + j) * 3
                    V.tensor_copy(r[:, :, 0:FE], a).then_inc(s_spc, 1)
                    dve.wait_ge(s_spc, n + 1)
                    V.tensor_tensor(a, a, r[:, :, 0:FE], ALU.subtract).then_inc(s_spc, 1)
                    dve.wait_ge(s_spc, n + 2)
                    V.tensor_copy(r[:, :, FE:2 * FE], a).then_inc(s_spc, 1)
                    dve.wait_ge(s_spc, n + 3)
                    V.tensor_tensor(r[:, :, 2 * FE:3 * FE], a, r[:, :, FE:2 * FE], ALU.subtract).then_inc(s_split, 1)
            split_features(0)
            with dve.Fori(1, NBLK // NSC) as q:
                split_features(q)

            dve.wait_ge(s_wts, 16 * len(WEIGHTS))
            link(V.tensor_copy(w1e_3[:, 0, :], w1e_t[:, :]))
            link(V.tensor_tensor(w1e_r[:, :], w1e_t[:, :], w1e_3[:, 0, :], ALU.subtract))
            link(V.tensor_copy(w1e_3[:, 1, :], w1e_r[:, :]))
            link(V.tensor_tensor(w1e_3[:, 2, :], w1e_r[:, :], w1e_3[:, 1, :], ALU.subtract))
            clear(passes[0], True)
            dve.wait_ge(s_meta[0], 16 * SLOTS4 * G)
            dve.wait_ge(s_fillt, 5)
            attention(passes[0])
            link(V.tensor_tensor(Wk[:, :, :], outv[:, :, 0:D], per_node(stat[:, 1, :]), ALU.mult))
            link(V.tensor_tensor(Wk[:, :, :], Wk[:, :, :], X[:, :, :], ALU.add))
            layer_norm()

            q1 = passes[1]
            clear(q1, False)
            dve.wait_ge(s_meta[1], 16 * SLOTS4 * G)

            dve.wait_ge(s_A[1], 10)
            split_nodes(Bt, D)

            def rows_of(t, g):
                return t[:, g.par, :].rearrange("p (j f) -> p j f", f=D)

            def add_source(g):
                wait_ring(dve, s_gather, NG, g, G)
                wait_done(dve, q1.hidden, g)
                wait_done(dve, q1.hi, g, back=2)
                wait_done(dve, q1.rest, g, back=2)
                V.tensor_tensor(rows_of(hsum, g), banks(2 + g.par)[:, 0:G * D].rearrange("p (j f) -> p j f", f=D),
                                xg[:, g.ring, :, VAL:VAL + D], ALU.add).then_inc(q1.hsum.sem, 1)

            def leave(g):
                wait_done(dve, q1.hi, g)
                wait_done(dve, q1.lo, g, back=2)
                V.scalar_tensor_tensor(rows_of(hres, g), rows_of(hsum, g), 0.0, hid[:, g.par, :, 0, 0:D],
                                       ALU.max, ALU.subtract).then_inc(q1.rest.sem, 1)

            def tail(g):
                wait_done(dve, q1.mid, g)
                V.tensor_tensor(hid[:, g.par, :, 2, 0:D], rows_of(hres, g), hid[:, g.par, :, 1, 0:D],
                                ALU.subtract).then_inc(q1.lo.sem, 1)

            def step(at):
                if at(0):
                    add_source(at(0))
                if at(2):
                    onehot(q1, at(2))
                if at(0):
                    leave(at(0))
                if at(-2):
                    add_sums(q1, at(-2), D + 1)
                if at(0):
                    tail(at(0))
            sweep(dve, step)
            dve.wait_ge(s_gate[1], 10)
            link(V.tensor_tensor(Wk[:, :, :], gates[:, :, 0:D], gates[:, :, 3 * D:4 * D], ALU.mult))
            V.tensor_tensor(Wk[:, :, :], Wk[:, :, :], gates[:, :, 2 * D:3 * D], ALU.add).then_inc(s_cand, 1)
            dve.wait_ge(s_tanh, 1)
            link(V.tensor_tensor(Wk[:, :, :], X[:, :, :], Wk2[:, :, :], ALU.subtract))
            link(V.tensor_tensor(Wk[:, :, :], Wk[:, :, :], gates[:, :, D:2 * D], ALU.mult))
            link(V.tensor_tensor(Wk[:, :, :], Wk[:, :, :], Wk2[:, :, :], ALU.add))
            link(V.tensor_tensor(Wk[:, :, :], Wk[:, :, :], X[:, :, :], ALU.add))
            layer_norm()

            q2 = passes[2]
            clear(q2, False)

            def weighted(g):
                wait_done(dve, q2.sum, g, back=SLOTS4)
                for j in range(G):
                    e = ds(g.k * G + j, 1)
                    last = V.tensor_scalar(OHW[:, g.ring, tile(j)], iota[:, :], meta1[:, e, M_LO], meta1[:, e, M_W],
                                           ALU.is_equal, ALU.mult)
                last.then_inc(q2.oh.sem, 1)

            def step(at):
                if at(-1):
                    add_sums(q2, at(-1), D)
                if at(1):
                    weighted(at(1))
            sweep(dve, step)
            done(q2.acc, dve)
            link(V.tensor_tensor(Wk[:, :, :], outv[:, :, 0:D], X[:, :, :], ALU.add))
            layer_norm()

            for i in range(2):
                if i == 1:
                    dve.wait_ge(s_oT[0][0], 5)
                clear(passes[3 + i], True)
                dve.wait_ge(s_qk[i][1], 5)
                split_nodes(qf, NV)
                attention(passes[3 + i])
                V.tensor_tensor(outv, outv, stat[:, 1, :].unsqueeze(2).broadcast_to([P, NT, NV]), ALU.mult)\
                    .then_inc(s_on[i], 1)
            dve.wait_ge(s_y[1][1], 5)
            link(V.tensor_tensor(Wk[:, :, :], Wk2[:, :, :], X[:, :, :], ALU.add))
            layer_norm()


def kernel(**inputs):
    import numpy as _np
    import concourse.bacc as _bacc
    from concourse import mybir as _mybir
    from concourse.bass_utils import run_bass_kernel_spmd as _run

    a = {k: _np.asarray(v) for k, v in inputs.items()}
    w1 = a["L1_gnn_W1"]
    arrays = {
        "x": a["x"], "src": a["src"], "dst": a["dst"], "attr": a["edge_attr_32"], "etype": a["edge_type_8"],
        "ew": a["edge_weight"], "ew1": a["edge_weight1"],
        "w1s": w1[:, 0:D].T, "w1d": _np.concatenate([w1[:, D:2 * D].T, a["L1_gnn_b1"][None]]),
        "w1e": w1[:, 2 * D:].T, "w2b": _np.concatenate([a["L1_gnn_W2"].T, a["L1_gnn_b2"][None]]),
        "wi": _np.concatenate([a["L1_gnn_w_ih"].T, a["L1_gnn_b_ih"][None]]),
        "wh": _np.concatenate([a["L1_gnn_w_hh"].T, a["L1_gnn_b_hh"][None]]),
        "xw_w": a["L2_gnn_W"].transpose(1, 0, 2).reshape(D, RELS * D),
    }
    for i in ("1", "2"):
        w = {k: a[f"L3_gnn_{k}{i}"] for k in ("Wq", "bq", "Wk", "bk", "Wv", "bv", "We", "Ws", "bs")}
        arrays["wq" + i] = w["Wq"]
        arrays["bq" + i] = w["bq"][:, None]
        arrays["ka" + i] = _np.concatenate([w["Wk"].T, w["We"].T, w["bk"][:, None]], axis=1)
        arrays["wva" + i] = _np.concatenate([w["Wv"], w["We"], w["bv"][None]])
        arrays["wsa" + i] = _np.concatenate([w["Ws"], w["bs"][None]])
    arrays = {f"in_{k}_dram": _np.ascontiguousarray(v) for k, v in arrays.items()}

    nc = _bacc.Bacc("TRN2", target_bir_lowering=False, num_devices=1)
    p = {k[3:-5]: nc.dram_tensor(k, v.shape, _mybir.dt.from_np(v.dtype), kind="ExternalInput").ap()
         for k, v in arrays.items()}
    f32 = _mybir.dt.float32
    out = nc.dram_tensor("out_dram", (NODES, D), f32, kind="ExternalOutput").ap()
    scratch = [nc.dram_tensor(n, s, f32, kind=SCRATCH_KIND).ap() for n, s in (
        ("edges_by_source", (NSLOT, R0)), ("edges_by_destination", (NSLOT, RF)), ("unit_nodes", (NPAD, 2 * D)),
        ("source_part", (NPAD, D)), ("relation_nodes", (RELS * NPAD, D)), ("conv1_nodes", (NPAD, D)),
        ("conv2_nodes", (NPAD, D)))]
    gnn_kernel(nc, *(p[k] for k in ("x", "src", "dst", "attr", "etype", "ew", "ew1", "w1s", "w1d", "w1e",
                                    "w2b", "wi", "wh", "xw_w")),
               *([p[k + "1"], p[k + "2"]] for k in ("wq", "bq", "ka", "wva", "wsa")), out, scratch)
    r = _run(nc, [arrays], core_ids=[0])
    return r.results[0]["out_dram"]
```

```python
import concourse.bass as bass
from concourse import mybir
from contextlib import ExitStack


NODES = 3125
EDGES = 103125
D = 64
FE = 32
RELS = 8
LN_EPS = 1e-5
NORM_EPS = 1e-12

P = 128
NT = -(-NODES // P)
NPAD = NT * P
LAST = NODES - (NT - 1) * P
G = 4
S = G * P
SLOTS4 = 4
NG = -(-((EDGES + NT * (S - 1)) // S) // 2) * 2
NGT = -(-NG // SLOTS4) * SLOTS4
NSLOT = NGT * S

EP, EC = 128, 810
EFULL = (EP - 1) * EC
ELAST = EDGES - EFULL
CB = 5
NSC = 3
NBLK = EC // CB
META_ROUNDS = 19
META_LOADS = (16 * META_ROUNDS * G, 16 * SLOTS4 * G)
assert NGT % META_ROUNDS == 0 and META_ROUNDS < NBLK // NSC
RC = CB * NSC
RANK_STEPS = 8
NB = NT + 1
assert RC * NB <= EC and EC % RC == 0
LAST_ROUNDS = ELAST // RC
assert ELAST % RC == 0 and EP * EC - EDGES <= NSLOT - NG * S

R0 = 2
FW = 3 * FE // 2
RF = FW + 5
M_SRC, M_REL, M_LO, M_W, M_A = range(5)
SCRATCH_KIND = "Internal"
XW_ = 130
VAL = D
NV = D + 2

MASKED = 2.0 ** 100
NEW_BUCKET = -2.0 ** 110
NO_BOUND = 2.0 ** 120


def gnn_kernel(nc, x, src, dst, attr, etype, ew, ew1, w1s, w1d, w1e, w2b, wi, wh, xw_w,
               wq, bq, ka, wva, wsa, out, scratch):
    f32, i32, bf16 = mybir.dt.float32, mybir.dt.int32, mybir.dt.bfloat16
    ALU, ACT, AX = mybir.AluOpType, mybir.ActivationFunctionType, mybir.AxisListType
    ds = bass.ds
    t_edge0, t_edge1, t_xn, t_a, t_rel, t_x3, t_h = scratch

    ctx = ExitStack()
    with ctx:
        def sb(name, shape, dt=f32):
            return ctx.enter_context(nc.sbuf_tensor(name, shape, dt))

        def sem(name):
            return ctx.enter_context(nc.semaphore(name))

        iota_i = sb("iota_i", [P, P], i32)
        iota = sb("iota", [P, P])
        part_i = sb("part_i", [P, 1], i32)
        part = sb("part", [P, 1])
        ident = sb("ident", [P, P])
        before = sb("before", [P, P])
        ones = sb("ones", [P, P])
        ident_h = sb("ident_h", [P, P], bf16)
        iota_h = sb("iota_h", [P, P], bf16)
        pick = sb("pick", [2 * G, G, P], bf16)
        pick_at = sb("pick_at", [2 * G, G])
        gnum = sb("gnum", [P, NG])
        vrow_i = sb("vrow_i", [P, NB], i32)
        vrow = sb("vrow", [P, NB])

        w1s_t = sb("w1s_t", [D, D])
        w1d_t = sb("w1d_t", [D + 1, D])
        w1e_t = sb("w1e_t", [3 * FE, D])
        w1e_r = sb("w1e_r", [3 * FE, D])
        w1e_3 = sb("w1e_3", [3 * FE, 3, D], bf16)
        w2b_t = sb("w2b_t", [D + 1, D])
        wi_t = sb("wi_t", [D + 1, 3 * D])
        wh_t = sb("wh_t", [D + 1, 3 * D])
        rel_t = sb("rel_t", [D, RELS * D])
        wq_t = [sb(f"wq_t{i}", [D, D]) for i in range(2)]
        bq_t = [sb(f"bq_t{i}", [D, 1]) for i in range(2)]
        ka_t = [sb(f"ka_t{i}", [D + 1, NV]) for i in range(2)]
        wva_t = [sb(f"wva_t{i}", [NV, D]) for i in range(2)]
        wsa_t = [sb(f"wsa_t{i}", [D + 1, D]) for i in range(2)]

        X = sb("X", [P, NT, D])
        Wk = sb("Wk", [P, NT, D])
        Wk2 = sb("Wk2", [P, NT, D])
        xT = sb("xT", [D + 1, NPAD])
        qT_all = sb("qT_all", [P, NPAD])
        qT = qT_all[0:NV, :]
        mT = sb("mT", [D + 1, NPAD])
        OUT = sb("OUT", [P, NT * NV])
        big = sb("big", [P, NT * 4 * D])
        stat = sb("stat", [P, 4, NT])
        Bt = big[:, 0:NT * D]
        qf = big[:, 0:NT * NV]
        rest = big[:, NT * 2 * D:NT * 2 * D + NT * NV]
        node3 = sb("node3", [P, NT * 3 * NV], bf16)

        sort_a = sb("sort_a", [P, 6 * EC])
        sort_b = sb("sort_b", [P, 7 * EC])

        def part_of(whole, i):
            return whole[0:EP, i * EC:(i + 1) * EC]
        mask, csum, hi_f = (part_of(sort_a, i) for i in range(3))
        part_key_i = part_of(sort_a, 3).bitcast(i32)
        key_i = [part_of(sort_a, 4 + i).bitcast(i32) for i in range(2)]
        key_f = [part_of(sort_b, i) for i in range(2)]
        lo_f = [part_of(sort_b, 2 + i) for i in range(2)]
        rel_f, w_in, a_in = (part_of(sort_b, 4 + i) for i in range(3))
        pos = [sb(f"pos{i}", [EP, EC]) for i in range(2)]
        rel_i = sb("rel_i", [EP, EC], i32)
        cnt = sb("cnt", [EP, NT])
        srt = sb("srt", [P, 6, NT])
        slot_at = sb("slot_at", [EP, 2, NB])
        srt_i = sb("srt_i", [P, NT], i32)
        zrow = sb("zrow", [P, NT])
        cmp = big[:, 0:NG * (NT - 1)]
        bucket_f = big[:, NG * (NT - 1):NG * NT]
        cap = [sb(f"cap{i}", [P, NG]) for i in range(2)]
        gnum_i = cap[0].bitcast(i32)
        bucket = [sb(f"bucket{i}", [1, NG], i32) for i in range(2)]
        attr_in = sb("attr_in", [EP, NSC, CB * FE])
        row0 = sb("row0", [EP, NSC, CB * R0])
        row1 = sb("row1", [EP, NSC, CB * RF])
        slot_i = sb("slot_i", [EP, NSC, CB], i32)
        FILL = NSLOT // P // 16
        fill = qT_all[:, 0:FILL * RF]

        meta0 = sb("meta0", [P, NGT * G, R0])
        MF = RF - FW
        meta1 = sort_a[:, 0:NGT * G * MF].rearrange("p (e f) -> p e f", f=MF)
        gidx = sb("gidx", [P, SLOTS4, G], i32)
        xg = sb("xg", [P, SLOTS4, G, XW_])
        rows = sb("rows", [P, SLOTS4, G * RF])
        OH = sb("OH", [P, SLOTS4, G, P], bf16)

        def of_b(a, n, *shape):
            v = sort_b[:, a:a + n]
            return v.rearrange("p (n s) -> p n s", n=shape[0]) if shape else v
        OHW = of_b(0, SLOTS4 * S, SLOTS4)
        OHT = of_b(2048, SLOTS4 * S // 2, SLOTS4).bitcast(bf16)
        pen = of_b(3072, S, 2).bitcast(bf16)
        sm = of_b(3584, S)
        hsum = of_b(4096, 2 * G * D, 2)
        hres = of_b(4608, 2 * G * D, 2)
        fT = sb("fT", [3 * FE, 2, S], bf16)
        prod = of_b(5120, 2 * G * NV, 2)
        score = sb("score", [P, 2, G])
        score2 = sb("score2", [P, 2, G, 2], bf16)
        scoreT = sb("scoreT", [2 * G, 2, P], bf16)
        less = sb("less", [P, 2, G])
        wgt = sb("wgt", [P, 2, G])
        ref_old = sb("ref_old", [P, 2])
        ref_new = sb("ref_new", [P, 2])
        ref2 = sb("ref2", [P, 2, 2], bf16)
        max_new = sb("max_new", [P, 2])
        fade = sb("fade", [P, SLOTS4])
        faded = sb("faded", [P, 2, NV])
        masked_b = sb("masked_b", [P, 1])
        hid = sb("hid", [P, 2, G, 3, D + 1], bf16)
        gates = big[:, :].rearrange("p (t f) -> p t f", f=4 * D)

        PS = ctx.enter_context(nc.psum_tensor("PS", [P, 8, 512], f32))

        def banks(b, n=1):
            return PS[:, b:b + n, :].rearrange("p b c -> p (b c)")

        def bank_h(b):
            return banks(b).bitcast(bf16)

        s_const = sem("constants_ready")
        s_iota = sem("iotas_written")
        s_wts = sem("weights_loaded")
        s_x = sem("x_loaded")
        s_empty = sem("places_without_edges_set")
        s_last = [sem(f"last_attr_block_loaded{j}") for j in range(NSC)]
        s_key = [sem(f"key{i}_loaded") for i in range(2)]
        s_rel = sem("edge_scalars_loaded")
        s_dch = sem("dve_step_done")
        s_cnt = [sem(f"counts{i}_ready") for i in range(2)]
        s_pre = [sem(f"prefixes{i}_ready") for i in range(2)]
        s_rank = sem("rank_step_done")
        s_pos = [sem(f"positions{i}_ready") for i in range(2)]
        s_bkt = [sem(f"buckets{i}_ready") for i in range(2)]
        s_fillt = sem("fill_tile_ready")
        s_fill0 = sem("edge_table0_cleared")
        s_fill1 = sem("edge_table1_cleared")
        s_pack = [sem(f"block{i}_packed") for i in range(2)]
        s_sc = [[sem(f"block{i}_scattered{j}") for j in range(NSC)] for i in range(2)]
        s_at = [sem(f"attr_block_loaded{j}") for j in range(NSC)]
        s_meta = [sem(f"meta{i}_loaded") for i in range(2)]

        class Count:
            def __init__(self, s, base):
                self.sem, self.base = s, base

        ALL = {n: sem(n) for n in ("idx_written", "onehot_written", "group_summed", "sums_added")}
        ATT = {n: sem(n) for n in (
            "attribute_written", "onehot_transposed", "onehot_copied", "penalty_written", "queries_gathered",
            "products_written", "scores_written", "scores_head", "scores_split", "scores_transposed",
            "scores_copied", "scores_spread", "old_reference_read", "new_max_ready", "reference_head",
            "reference_split", "reference_ready", "sums_stored", "reference_gathered",
            "score_less_reference", "weight_ready", "fade_ready", "weighted_onehot")}
        MSG = {n: sem("msg_" + n) for n in (
            "onehot_transposed", "onehot_copied", "features_transposed", "features_copied",
            "hidden_ready", "hidden_added", "head_ready", "rest_ready", "middle_ready", "tail_ready")}
        s_gather = [sem(f"rows_gathered{j}") for j in range(SLOTS4)]
        s_rows = [sem(f"features_loaded{j}") for j in range(SLOTS4)]
        s_table = [sem(f"table{i}_in_dram") for i in range(5)]

        class Pass:
            def __init__(self, i, attention):
                self.i = i
                self.start = s_table[i]
                self.idx = Count(ALL["idx_written"], i * NG)
                self.oh = Count(ALL["onehot_written"], i * NG)
                self.sum = Count(ALL["group_summed"], i * NG)
                self.acc = Count(ALL["sums_added"], i * NG)
                if attention is not None:
                    (self.acol, self.toh, self.ohT, self.pen, self.qg, self.prod, self.score, self.s_hi, self.s2,
                     self.sT, self.sTc, self.spread, self.ro, self.mn, self.r_hi, self.r2, self.rn, self.stored,
                     self.rg, self.less, self.w, self.fade, self.ohw) = (
                        Count(s, attention * NG) for s in ATT.values())
                    if attention:
                        self.acol = Count(ATT["attribute_written"], (attention - 1) * NG)
                    self.K = D if attention == 0 else NV
                    self.key0 = 0 if attention == 0 else VAL
                if i == 1:
                    (self.toh, self.ohT, self.tf, self.fT, self.hidden, self.hsum, self.hi, self.rest,
                     self.mid, self.lo) = (Count(s, 0) for s in MSG.values())
                self.meta = meta0 if i == 0 else meta1
                self.key = 0 if i == 0 else 1
                self.m_idx = (0, M_SRC, M_REL, M_SRC, M_SRC)[i]
                self.m_lo = 1 if i == 0 else M_LO

        passes = [Pass(0, 0), Pass(1, None), Pass(2, None), Pass(3, 1), Pass(4, 2)]

        def pair(name):
            return sem(name + "_on_pe"), sem(name + "_copied")
        s_sq = sem("norm_squares_ready")
        s_nrm = sem("norms_ready")
        s_hn = sem("unit_nodes_ready")
        s_n3 = sem("node_rows_split")
        s_split = sem("features_split")
        s_spc = sem("features_split_step")
        s_var = sem("variances_ready")
        s_std = sem("deviations_ready")
        s_X = sem("nodes_ready")
        s_xT = [pair(f"nodes_transposed{i}") for i in range(3)]
        s_A = pair("message_tables")
        s_aT = pair("sums_transposed")
        s_mT = pair("messages")
        s_gate = pair("gates")
        s_cand = sem("candidate_input_ready")
        s_tanh = sem("candidate_ready")
        s_xw = pair("relation_tables")
        s_xwo = [sem(f"relation_table_stored{i}") for i in range(4)]
        s_wqT = pair("query_weights_transposed")
        s_fold = pair("query_weights_folded")
        s_qk = [pair(f"folded_queries{i}") for i in range(2)]
        s_on = [sem(f"attention_normalised{i}") for i in range(2)]
        s_oT = [pair(f"attention_transposed{i}") for i in range(2)]
        s_y = [pair(f"conv_out{i}") for i in range(2)]
        s_hT = pair("hidden_transposed")
        s_out = sem("output_written")

        class Group:
            def __init__(self, k, c, q):
                self.k, self.ring, self.uses = k, c % SLOTS4, q + c // SLOTS4
                self.par = c % 2
                self.static = isinstance(k, int)

        def sweep(e, step):
            def peeled(t):
                step(lambda off: Group(t + off, (t + off) % SLOTS4, (t + off) // SLOTS4)
                     if 0 <= t + off < NG else None)
            for t in range(-2, SLOTS4):
                peeled(t)
            with e.Fori(1, NG // SLOTS4 - 1) as q:
                for c in range(SLOTS4):
                    step(lambda off: Group(q * SLOTS4 + (c + off), c + off, q))
            for t in range((NG // SLOTS4 - 1) * SLOTS4, NG + 3):
                peeled(t)

        def wait_done(e, count, g, back=0):
            if g.static and count.base == 0 and g.k < back:
                return
            e.wait_ge(count.sem, g.k + (count.base + 1 - back))

        def wait_ring(e, sems, passed, g, n):
            before = passed * len(range(g.ring, NG, SLOTS4))
            e.wait_ge(sems[g.ring], g.uses * (16 * n) + (before + 1) * 16 * n)

        def load_meta(e, i, first, n, j):
            meta, table, w0, w1 = ((meta0, t_edge0, 0, R0), (meta1, t_edge1, FW, RF))[i]
            tv = table.rearrange("(g p j) f -> p g j f", p=P, j=G)
            mv = meta[:, :, :].rearrange("p (g j) f -> p g j f", j=G)
            e.dma_start(mv[:, ds(first, n), j, :], tv[:, ds(first, n), j, w0:w1]).then_inc(s_meta[i], 16)

        def bucket_of(e, q, g):
            return e.value_load(bucket[q.key][0:1, ds(g.k, 1)], min_val=0, max_val=NT - 1)

        def tile(t):
            return slice(t * P, (t + 1) * P)

        def done(s, e):
            e.wait_ge(s.sem, s.base + NG)

        wqT = Wk2[0:D, :, :].rearrange("p t f -> p (t f)")[:, 0:2 * (D + 1)].rearrange("p (i f) -> p i f", i=2)
        WEIGHTS = [(w1s_t, w1s), (w1d_t, w1d), *((w1e_t[i * FE:(i + 1) * FE, :], w1e) for i in range(3)), (w2b_t, w2b), (wi_t, wi), (wh_t, wh), (rel_t, xw_w)]
        for i in range(2):
            WEIGHTS += [(wq_t[i], wq[i]), (bq_t[i], bq[i]), (ka_t[i][0:D, :], ka[i]), (wva_t[i], wva[i]), (wsa_t[i], wsa[i])]

        block = ctx.enter_context(nc.Block())

        @block.gpsimd
        def _(pool):
            for i in range(2):
                pool.memset(key_i[1 - i][:, :], NPAD).then_inc(s_empty, 1)
            pool.iota(iota_i[:, :], pattern=[[1, P]], base=0, channel_multiplier=0)
            pool.iota(part_i[:, :], pattern=[[0, 1]], base=0, channel_multiplier=1)
            pool.iota(vrow_i[:, :], pattern=[[1, NB]], base=0, channel_multiplier=0)
            pool.iota(gnum_i[:, :], pattern=[[1, NG]], base=0, channel_multiplier=0).then_inc(s_iota, 1)
            pool.memset(rel_i[:, :], 0)
            pool.memset(w_in[:, :], 0.0)
            pool.memset(a_in[:, :], 0.0).then_inc(s_empty, 1)
            pool.memset(fill[:, :], 0.0).then_inc(s_fillt, 1)
            pool.wait_ge(s_fillt, 1)
            pool.memset(fill[:, :].rearrange("p (r f) -> p r f", f=RF)[:, :, FW + M_LO:FW + M_LO + 1], -1.0)\
                .then_inc(s_fillt, 1)
            pool.memset(xg[:, :, :, :], 0.0).then_inc(s_fillt, 1)
            pool.wait_ge(s_fillt, 3)
            pool.memset(xg[:, :, :, XW_ - 1:XW_], 1.0).then_inc(s_fillt, 1)
            pool.memset(meta0[:, :, 0:1], 0.0)
            pool.memset(meta0[:, :, 1:2], -1.0).then_inc(s_fillt, 1)

            for i, (row, width, table, cleared, nfill) in enumerate(
                    ((row0, R0, t_edge0, s_fill0, 1), (row1, RF, t_edge1, s_fill1, 16))):
                pool.wait_ge(cleared, 16 * nfill)

                def scatter(q):
                    for j in range(NSC):
                        if i == 1:
                            pool.wait_ge(s_split, q * NSC + (j + 1))
                        pool.wait_ge(s_pack[i], q * NSC + (j + 1))
                        pool.nop(nofuse=True)
                        for c in range(CB):
                            pool.indirect_dma_start(
                                out=table[:, :], in_=row[:, j, c * width:(c + 1) * width], in_offset=None,
                                out_offset=bass.IndirectOffsetOnAxis(ap=slot_i[:, j, c:c + 1], axis=0))\
                                .then_inc(s_sc[i][j], 16)
                scatter(0)
                with pool.Fori(1, NBLK // NSC) as q:
                    scatter(q)

            for i, (q, table, cols) in enumerate(zip(
                    passes, (t_xn, t_a, t_rel, t_x3, t_h),
                    (slice(0, 2 * D), *[slice(VAL, VAL + D)] * 4))):
                pool.wait_ge(q.start, 16 * (NT if i == 2 else 1))

                def gather(g):
                    wait_done(pool, q.idx, g)
                    pool.nop(nofuse=True)
                    for j in range(G):
                        pool.indirect_dma_start(
                            out=xg[:, g.ring, j, cols], out_offset=None, in_=table[:, :],
                            in_offset=bass.IndirectOffsetOnAxis(ap=gidx[:, g.ring, j:j + 1], axis=0))\
                            .then_inc(s_gather[g.ring], 16)
                sweep(pool, lambda at: at(0) and gather(at(0)))

        @block.sync
        def _(sp):
            def load_edges(tile_, values, loaded):
                sp.dma_start(tile_[0:EP - 1, :], values[0:EFULL].rearrange("(p c) -> p c", c=EC)).then_inc(loaded, 16)
                sp.dma_start(tile_[EP - 1:EP, 0:ELAST], values[EFULL:EDGES].rearrange("(p c) -> p c", p=1))\
                    .then_inc(loaded, 16)
            for i, k in ((1, dst), (0, src)):
                sp.wait_ge(s_empty, 2 - i)
                load_edges(key_i[i], k, s_key[i])
            sp.wait_ge(s_X, 1)
            sp.dma_start(X[:, 0:NT - 1, :], x[0:(NT - 1) * P, :].rearrange("(t p) f -> p t f", p=P)).then_inc(s_x, 16)
            sp.dma_start(X[0:LAST, NT - 1, :], x[(NT - 1) * P:NODES, :]).then_inc(s_x, 16)
            for t, d in WEIGHTS:
                sp.dma_start(t[:, :], d).then_inc(s_wts, 16)
            sp.wait_ge(s_empty, 3)
            load_edges(rel_i, etype, s_rel)
            load_edges(w_in, ew, s_rel)
            load_edges(a_in, ew1.rearrange("e o -> (e o)"), s_rel)
            sp.wait_ge(s_fillt, 5)
            sp.dma_start(t_edge0.rearrange("(p r) f -> p (r f)", p=P),
                         meta0[:, :, :].rearrange("p r f -> p (r f)")).then_inc(s_fill0, 16)
            e1 = t_edge1.rearrange("(p r) f -> p (r f)", p=P)
            for i in range(16):
                sp.wait_ge(s_pack[0], NSC * (i + 1))
                sp.dma_start(e1[:, i * FILL * RF:(i + 1) * FILL * RF], fill[:, :]).then_inc(s_fill1, 16)

            at_v = attr[0:EFULL, :].rearrange("(p c) f -> p (c f)", c=EC)
            at_last = attr[EFULL:EDGES, :].rearrange("(p c) f -> p (c f)", p=1)

            def load_attr(q, last):
                for j in range(NSC):
                    if not isinstance(q, int):
                        sp.wait_ge(s_split, q * NSC + (j + 1 - NSC))
                    cols = ds((q * NSC + j) * (CB * FE), CB * FE)
                    sp.dma_start(attr_in[0:EP - 1, j, :], at_v[:, cols]).then_inc(s_at[j], 16)
                    if last:
                        sp.dma_start(attr_in[EP - 1:EP, j, :], at_last[:, cols]).then_inc(s_last[j], 16)
            load_attr(0, True)
            with sp.Fori(1, LAST_ROUNDS) as q:
                load_attr(q, True)
            with sp.Fori(LAST_ROUNDS, NBLK // NSC) as q:
                load_attr(q, False)

            sp.wait_ge(s_hn, 1)
            sp.dma_start(t_xn.rearrange("(t p) f -> p t f", p=P),
                         big[:, 0:NT * 2 * D].rearrange("p (t f) -> p t f", t=NT)).then_inc(passes[0].start, 16)

            for j in range(NSC):
                sp.wait_ge(s_sc[1][j], 16 * EC // NSC)
            for i in range(SLOTS4):
                for j in range(G):
                    sp.wait_ge(passes[0].idx.sem, (i * G + j + 1) * SLOTS4)
                    load_meta(sp, 1, i * (NGT // SLOTS4), NGT // SLOTS4, j)

            sp.wait_ge(s_A[1], 5)
            sp.dma_start(t_a.rearrange("(t p) f -> p t f", p=P), Wk[:, :, :]).then_inc(passes[1].start, 16)
            q1 = passes[1]
            rv = t_edge1.rearrange("(g p j) f -> g p (j f)", p=P, j=G)

            def load_rows(g):
                wait_done(sp, q1.tf, g, back=SLOTS4)
                sp.dma_start(rows[:, g.ring, :], rv[ds(g.k, 1), :, :].rearrange("a p f -> p (a f)"))\
                    .then_inc(s_rows[g.ring], 16)
            sweep(sp, lambda at: at(0) and load_rows(at(0)))

            xwv = t_rel.rearrange("(r t p) f -> t p r f", r=RELS, p=P)
            for t in range(NT):
                sp.wait_ge(s_xw[1], t + 1)
                sp.dma_start(xwv[t, :, :, :], big[:, (t % 4) * 512:(t % 4 + 1) * 512]
                             .rearrange("p (r f) -> p r f", r=RELS)).then_inc(s_xwo[t % 4], 16)
            for j in range(4):
                sp.wait_ge(s_xwo[j], 16 * len(range(j, NT, 4)))
            sp.sem_inc(passes[2].start, 16 * NT)

            sp.wait_ge(s_X, 4)
            sp.dma_start(t_x3.rearrange("(t p) f -> p t f", p=P), X[:, :, :]).then_inc(passes[3].start, 16)
            sp.wait_ge(s_y[0][1], 5)
            sp.dma_start(t_h.rearrange("(t p) f -> p t f", p=P), Wk2[:, :, :]).then_inc(passes[4].start, 16)

            sp.wait_ge(s_X, 5)
            sp.dma_start(out[0:(NT - 1) * P, :].rearrange("(t p) f -> p t f", p=P), X[:, 0:NT - 1, :]).then_inc(s_out, 16)
            sp.dma_start(out[(NT - 1) * P:NODES, :], X[0:LAST, NT - 1, :]).then_inc(s_out, 16)
            sp.wait_ge(s_out, 32)

        @block.tensor
        def _(pe):
            mm, tr = nc.tensor.matmul, nc.tensor.transpose
            pe.wait_ge(s_const, 1)
            for i in range(2):
                pe.wait_ge(s_cnt[i], 1)
                mm(banks(7)[:, 0:NT], before[0:EP, :], cnt[:, :], start=True, stop=True)
                mm(banks(7)[:, 32:32 + NT], ones[0:EP, :], cnt[:, :], start=True, stop=True).then_inc(s_pre[i], 1)

            def transposes(source, width, on_pe, copied):
                for b in range(5):
                    if b >= 2:
                        pe.wait_ge(copied, b - 1)
                    for j in range(5):
                        last = tr(banks(2 * (b % 2), 2)[0:width, tile(j)], source(5 * b + j), ident[:, :])
                    last.then_inc(on_pe, 1)

            def project(weight, source, rows, width, on_pe, copied):
                for b in range(5):
                    if b >= 2:
                        pe.wait_ge(copied, b - 1)
                    for c0, c1 in ((0, 512), (512, 5 * P)):
                        last = mm(banks(4 + 2 * (b % 2), 2)[0:width, c0:c1], weight,
                                  source[0:rows, b * 5 * P + c0:b * 5 * P + c1], start=True, stop=True)
                    last.then_inc(on_pe, 1)

            def turn_onehot(q, bank, g):
                wait_done(pe, q.oh, g)
                wait_done(pe, q.ohT, g, back=1)
                for j in range(G):
                    last = tr(bank_h(bank)[:, tile(j)], OH[:, g.ring, j, :], ident_h[:, :])
                last.then_inc(q.toh.sem, 1)

            def attention(q):
                def queries(g, b):
                    wait_done(pe, q.ohT, g)
                    wait_done(pe, q.prod, g, back=1)
                    pe.nop(nofuse=True)
                    for j in range(G):
                        for part_ in range(3):
                            last = mm(banks(0)[:, j * q.K:(j + 1) * q.K], OHT[:, g.ring, tile(j)],
                                      node3[:, ds(b * (3 * q.K) + part_ * q.K, q.K)],
                                      start=(part_ == 0), stop=(part_ == 2))
                    last.then_inc(q.qg.sem, 1)

                def sums(g):
                    wait_done(pe, q.ohw, g)
                    wait_done(pe, q.acc, g, back=2)
                    for j in range(G):
                        last = mm(banks(6 + g.par)[:, 0:NV], OHW[:, g.ring, tile(j)], xg[:, g.ring, j, VAL:XW_],
                                  start=(j == 0), stop=(j == G - 1))
                    last.then_inc(q.sum.sem, 1)

                def references(g):
                    wait_done(pe, q.r2, g)
                    wait_done(pe, q.less, g, back=1)
                    for j in range(G):
                        for part_ in range(2):
                            last = mm(banks(3)[:, j:j + 1], OHT[:, g.ring, tile(j)], ref2[:, g.par, part_:part_ + 1],
                                      start=(part_ == 0), stop=(part_ == 1))
                    last.then_inc(q.rg.sem, 1)

                def turn_scores(g):
                    wait_done(pe, q.s2, g)
                    wait_done(pe, q.sTc, g, back=1)
                    tr(bank_h(2)[0:2 * G, 0:P], score2[:, g.par, :, :].rearrange("p j h -> p (j h)"),
                       ident_h[:, :]).then_inc(q.sT.sem, 1)

                def spread(g):
                    wait_done(pe, q.sTc, g)
                    wait_done(pe, q.mn, g, back=2)
                    for j in range(G):
                        last = mm(banks(4 + g.par)[:, tile(j)], pick[:, j, :], scoreT[:, g.par, :],
                                  start=True, stop=True)
                    last.then_inc(q.spread.sem, 1)

                def step(at):
                    b = bucket_of(pe, q, at(1)) if at(1) else None
                    if at(-2):
                        sums(at(-2))
                    if at(-1):
                        references(at(-1))
                    if at(0):
                        turn_scores(at(0))
                    if at(1):
                        queries(at(1), b)
                    if at(0):
                        spread(at(0))
                    if at(2):
                        turn_onehot(q, 1, at(2))
                sweep(pe, step)

            pe.wait_ge(s_wts, 16 * len(WEIGHTS))
            for i in range(2):
                tr(banks(4 + i)[0:D, 0:D], wq_t[i][:, :], ident[0:D, 0:D]).then_inc(s_wqT[0], 1)
            for i in range(2):
                pe.wait_ge(s_wqT[1], 2 * i + 2)
                mm(banks(2 + i)[0:D + 1, 0:NV], wqT[:, i, :], ka_t[i][0:D, :], start=True, stop=True).then_inc(s_fold[0], 1)
            pe.wait_ge(s_fold[1], 2)

            pe.wait_ge(s_n3, 1)
            attention(passes[0])

            pe.wait_ge(s_X, 2)
            pe.wait_ge(s_wts, 16 * len(WEIGHTS))
            transposes(lambda t: X[:, t, :], D, *s_xT[0])
            pe.wait_ge(s_xT[0][1], 5)
            for b in range(10):
                if b >= 4:
                    pe.wait_ge(s_A[1], b - 3)
                rows_in, w = (D, w1s_t) if b < 5 else (D + 1, w1d_t)
                for j in range(5):
                    last = mm(banks(4 + b % 4)[:, j * D:(j + 1) * D], xT[0:rows_in, tile(5 * (b % 5) + j)], w[:, :],
                              start=True, stop=True)
                last.then_inc(s_A[0], 1)
            pe.wait_ge(s_A[1], 10)
            pe.wait_ge(s_n3, 2)
            q = passes[1]

            def turn_features(g):
                wait_ring(pe, s_rows, 0, g, 1)
                wait_done(pe, q.fT, g, back=1)
                for j in range(G):
                    last = tr(bank_h(0)[0:3 * FE, tile(j)],
                              rows[:, g.ring, j * RF:j * RF + FW].bitcast(bf16), ident_h[:, :])
                last.then_inc(q.tf.sem, 1)

            def hidden(g):
                b = bucket_of(pe, q, g)
                wait_done(pe, q.ohT, g)
                wait_done(pe, q.fT, g)
                wait_done(pe, q.hsum, g, back=2)
                pe.nop(nofuse=True)
                for j in range(G):
                    o = banks(2 + g.par)[:, j * D:(j + 1) * D]
                    for part_ in range(3):
                        mm(o, OHT[:, g.ring, tile(j)], node3[:, ds(b * (3 * D) + part_ * D, D)],
                           start=(part_ == 0), stop=False)
                    for part_ in range(3):
                        last = mm(o, fT[:, g.par, tile(j)], w1e_3[:, part_, :], start=False, stop=(part_ == 2))
                last.then_inc(q.hidden.sem, 1)

            def message_sums(g):
                wait_done(pe, q.lo, g)
                wait_done(pe, q.acc, g, back=2)
                for j in range(G):
                    for part_ in range(3):
                        last = mm(banks(6 + g.par)[:, 0:D + 1], OH[:, g.ring, j, :], hid[:, g.par, j, part_, :],
                                  start=(j + part_ == 0), stop=(j == G - 1 and part_ == 2))
                last.then_inc(q.sum.sem, 1)

            def step(at):
                if at(0):
                    hidden(at(0))
                if at(1):
                    turn_onehot(q, 1, at(1))
                    turn_features(at(1))
                if at(-1):
                    message_sums(at(-1))
            sweep(pe, step)

            done(q.acc, pe)
            transposes(lambda t: OUT[:, t * NV:t * NV + D + 1], D + 1, *s_aT)
            pe.wait_ge(s_aT[1], 5)
            project(w2b_t[:, :], qT, D + 1, D, *s_mT)
            pe.wait_ge(s_mT[1], 5)
            for b in range(5):
                if b >= 2:
                    pe.wait_ge(s_gate[1], 2 * (b - 1))
                for j in range(5):
                    o = banks(3 * (b % 2), 3)[:, j * 4 * D:(j + 1) * 4 * D]
                    mm(o[:, 0:3 * D], mT[:, tile(5 * b + j)], wi_t[:, :], start=True, stop=False, skip_group_check=True)
                    mm(o[:, 0:2 * D], xT[:, tile(5 * b + j)], wh_t[:, 0:2 * D], start=False, stop=True, skip_group_check=True)
                    last = mm(o[:, 3 * D:4 * D], xT[:, tile(5 * b + j)], wh_t[:, 2 * D:3 * D], start=True, stop=True, skip_group_check=True)
                last.then_inc(s_gate[0], 1)

            pe.wait_ge(s_X, 3)
            transposes(lambda t: X[:, t, :], D, *s_xT[1])
            pe.wait_ge(s_xT[1][1], 5)
            for t in range(NT):
                if t >= 4:
                    pe.wait_ge(s_xw[1], t - 3)
                mm(banks(4 + t % 4), xT[0:D, tile(t)], rel_t[:, :], start=True, stop=True).then_inc(s_xw[0], 1)
            pe.wait_ge(s_xw[1], NT)
            q = passes[2]

            def relation_sums(g):
                wait_ring(pe, s_gather, 2, g, G)
                wait_done(pe, q.oh, g)
                wait_done(pe, q.acc, g, back=2)
                for j in range(G):
                    last = mm(banks(6 + g.par)[:, 0:D], OHW[:, g.ring, tile(j)], xg[:, g.ring, j, VAL:VAL + D],
                              start=(j == 0), stop=(j == G - 1))
                last.then_inc(q.sum.sem, 1)
            sweep(pe, lambda at: at(0) and relation_sums(at(0)))

            for i in range(2):
                if i == 0:
                    pe.wait_ge(s_X, 4)
                    transposes(lambda t: X[:, t, :], D, *s_xT[2])
                    pe.wait_ge(s_xT[2][1], 5)
                else:
                    pe.wait_ge(s_y[0][1], 5)
                    transposes(lambda t: Wk2[:, t, :], D, *s_hT)
                    pe.wait_ge(s_hT[1], 5)
                for b in range(5):
                    if b >= 2:
                        pe.wait_ge(s_qk[i][1], b - 1)
                    for j in range(5):
                        last = mm(banks(2 + b % 2)[:, j * NV:(j + 1) * NV], xT[:, tile(5 * b + j)], ka_t[i][:, :],
                                  start=True, stop=True)
                    last.then_inc(s_qk[i][0], 1)
                pe.wait_ge(s_n3, 3 + i)
                attention(passes[3 + i])
                pe.wait_ge(s_on[i], 1)
                transposes(lambda t: OUT[:, t * NV:(t + 1) * NV], NV, *s_oT[i])
                pe.wait_ge(s_oT[i][1], 5)
                for b in range(5):
                    if b >= 2:
                        pe.wait_ge(s_y[i][1], b - 1)
                    for j in range(5):
                        o = banks(4 + b % 2)[:, j * D:(j + 1) * D]
                        mm(o, qT[:, tile(5 * b + j)], wva_t[i][:, :], start=True, stop=False)
                        last = mm(o, xT[:, tile(5 * b + j)], wsa_t[i][:, :], start=False, stop=True)
                    last.then_inc(s_y[i][0], 1)

        @block.scalar
        def _(act):
            A = nc.scalar.activation

            for i in range(2):
                if i == 1:
                    act.wait_ge(s_sq, 1)
                    A(stat[:, 1, :], stat[:, 0, :], ACT.Sqrt).then_inc(s_nrm, 1)
                    for j in range(NSC):
                        act.wait_ge(s_sc[0][j], 16 * EC // NSC)

                def pack(q):
                    for j in range(NSC):
                        if not isinstance(q, int):
                            act.wait_ge(s_sc[i][j], q * (16 * CB))
                            act.nop(nofuse=True)
                        if j == 0:
                            act.wait_ge(s_pos[i], q + 1)
                            act.nop(nofuse=True)
                        c = ds((q * NSC + j) * CB, CB)
                        if i == 0:
                            r = row0[:, j, :].rearrange("p (c f) -> p c f", f=R0)
                            A(r[:, :, 0:1], key_f[1][:, c].unsqueeze(2), ACT.Copy)
                            A(r[:, :, 1:2], lo_f[0][:, c].unsqueeze(2), ACT.Copy)
                        else:
                            r = row1[:, j, :].rearrange("p (c f) -> p c f", f=RF)
                            for m, src_ in ((M_SRC, key_f[0]), (M_REL, rel_f), (M_LO, lo_f[1]), (M_W, w_in), (M_A, a_in)):
                                A(r[:, :, FW + m:FW + m + 1], src_[:, c].unsqueeze(2), ACT.Copy)
                        A(slot_i[:, j, :], pos[i][:, c], ACT.Copy).then_inc(s_pack[i], 1)
                pack(0)
                done_rounds = 1
                if i == 1:
                    done_rounds = META_ROUNDS + 1
                    with act.Fori(1, done_rounds) as q:
                        pack(q)
                        for j in range(G):
                            load_meta(act, 0, q * (NGT // META_ROUNDS) - NGT // META_ROUNDS, NGT // META_ROUNDS, j)
                with act.Fori(done_rounds, NBLK // NSC) as q:
                    pack(q)

            def copy_pairs(dst_, width, on_pe, copied, func=ACT.Copy, first=4, **kw):
                for b in range(5):
                    act.wait_ge(on_pe, b + 1)
                    A(dst_[0:width, b * 5 * P:(b + 1) * 5 * P], banks(first + 2 * (b % 2), 2)[0:width, 0:5 * P],
                      func, **kw).then_inc(copied, 1)

            def prepare_first(q):
                act.wait_ge(s_meta[q.key], META_LOADS[q.key])
                if q.i:
                    done(passes[q.i - 1].sum, act)
                for k in range(SLOTS4):
                    prepare(q, Group(k, k, 0))

            def prepare_next(q, g):
                if g and not (g.static and g.k < SLOTS4):
                    prepare(q, g)

            def prepare(q, g):
                wait_done(act, q.sum, g, back=SLOTS4)
                act.nop(nofuse=True)
                A(gidx[:, g.ring, :], q.meta[:, ds(g.k * G, G), q.m_idx], ACT.Copy).then_inc(q.idx.sem, 1)
                if q.i >= 3:
                    A(xg[:, g.ring, :, VAL + D], q.meta[:, ds(g.k * G, G), M_A], ACT.Copy).then_inc(q.acol.sem, 1)

            def copy_onehot(q, g):
                wait_done(act, q.toh, g)
                if q.i == 1:
                    wait_done(act, q.sum, g, back=SLOTS4)
                else:
                    wait_done(act, q.rg, g, back=SLOTS4)
                    wait_done(act, q.pen, g, back=SLOTS4)
                A(OHT[:, g.ring, :], bank_h(1)[:, 0:S], ACT.Copy).then_inc(q.ohT.sem, 1)

            def attention(q):
                def penalty(g):
                    wait_done(act, q.ohT, g)
                    wait_done(act, q.mn, g, back=2)
                    A(pen[:, g.par, :], OHT[:, g.ring, :], ACT.Identity, scale=MASKED, bias=masked_b[:, 0:1])\
                        .then_inc(q.pen.sem, 1)

                def fades(g):
                    wait_done(act, q.rn, g)
                    wait_done(act, q.acc, g, back=SLOTS4)
                    A(fade[:, g.ring:g.ring + 1], ref_new[:, g.par:g.par + 1], ACT.Exp, scale=-1.0,
                      bias=ref_old[:, g.par:g.par + 1]).then_inc(q.fade.sem, 1)

                def copy_scores(g):
                    wait_done(act, q.sT, g)
                    wait_done(act, q.spread, g, back=2)
                    A(scoreT[:, g.par, :], bank_h(2)[0:2 * G, 0:P], ACT.Copy).then_inc(q.sTc.sem, 1)

                def weights(g):
                    wait_done(act, q.less, g)
                    wait_done(act, q.ohw, g, back=2)
                    A(wgt[:, g.par, :], less[:, g.par, :], ACT.Exp).then_inc(q.w.sem, 1)

                def store(g):
                    b = bucket_of(act, q, g)
                    wait_done(act, q.acc, g)
                    wait_done(act, q.stored, g, back=1)
                    act.nop(nofuse=True)
                    A(OUT[:, ds(b * NV, NV)], faded[:, g.par, :], ACT.Copy).then_inc(q.stored.sem, 1)

                def step(at):
                    prepare_next(q, at(2))
                    if at(0):
                        copy_scores(at(0))
                    if at(-1):
                        weights(at(-1))
                        fades(at(-1))
                    if at(-3):
                        store(at(-3))
                    if at(1):
                        penalty(at(1))
                    if at(2):
                        copy_onehot(q, at(2))
                sweep(act, step)

            def deviations():
                act.wait_ge(s_var, deviations.n)
                A(stat[:, 3, :], stat[:, 2, :], ACT.Sqrt).then_inc(s_std, 1)
                deviations.n += 1
            deviations.n = 1

            act.wait_ge(s_bkt[0], 1)
            act.wait_ge(s_pack[1], NBLK)
            prepare_first(passes[0])
            attention(passes[0])
            deviations()

            prepare_first(passes[1])
            copy_pairs(xT, D, *s_xT[0], first=0)
            for b in range(10):
                act.wait_ge(s_A[0], b + 1)
                source = banks(4 + b % 4)[:, 0:5 * D]
                if b < 5:
                    A(Wk[:, 5 * b:5 * b + 5, :], source.rearrange("p (t f) -> p t f", f=D), ACT.Copy).then_inc(s_A[1], 1)
                else:
                    A(Bt[:, 5 * (b - 5) * D:5 * (b - 4) * D], source, ACT.Copy).then_inc(s_A[1], 1)
            q = passes[1]

            def copy_features(g):
                wait_done(act, q.tf, g)
                wait_done(act, q.hidden, g, back=2)
                A(fT[:, g.par, :], bank_h(0)[0:3 * FE, 0:S], ACT.Copy).then_inc(q.fT.sem, 1)

            def rows_of(t, g):
                return t[:, g.par, :].rearrange("p (j f) -> p j f", f=D)

            def head(g):
                wait_done(act, q.hsum, g)
                wait_done(act, q.sum, g, back=2)
                A(hid[:, g.par, :, 0, 0:D], rows_of(hsum, g), ACT.Relu).then_inc(q.hi.sem, 1)

            def middle(g):
                wait_done(act, q.rest, g)
                A(hid[:, g.par, :, 1, 0:D], rows_of(hres, g), ACT.Copy).then_inc(q.mid.sem, 1)

            def step(at):
                prepare_next(q, at(2))
                if at(0):
                    head(at(0))
                if at(1):
                    copy_onehot(q, at(1))
                if at(0):
                    middle(at(0))
                if at(1):
                    copy_features(at(1))
            sweep(act, step)
            prepare_first(passes[2])
            copy_pairs(qT, D + 1, *s_aT, first=0)
            copy_pairs(mT, D, *s_mT)
            for b in range(5):
                act.wait_ge(s_gate[0], b + 1)
                g4 = banks(3 * (b % 2), 3)[:, 0:5 * 4 * D].rearrange("p (t f) -> p t f", f=4 * D)
                A(gates[:, 5 * b:5 * b + 5, 0:2 * D], g4[:, :, 0:2 * D], ACT.Sigmoid).then_inc(s_gate[1], 1)
                A(gates[:, 5 * b:5 * b + 5, 2 * D:4 * D], g4[:, :, 2 * D:4 * D], ACT.Copy).then_inc(s_gate[1], 1)
                act.wait_ge(s_cand, b + 1)
                A(Wk2[:, 5 * b:5 * b + 5, :], Wk[:, 5 * b:5 * b + 5, :], ACT.Tanh).then_inc(s_tanh, 1)
            deviations()

            copy_pairs(xT, D, *s_xT[1], first=0)
            for t in range(NT):
                act.wait_ge(s_xw[0], t + 1)
                if t >= 4:
                    act.wait_ge(s_xwo[t % 4], 16 * (t // 4))
                A(big[:, (t % 4) * 512:(t % 4 + 1) * 512], banks(4 + t % 4), ACT.Copy).then_inc(s_xw[1], 1)
            sweep(act, lambda at: prepare_next(passes[2], at(2)))
            prepare_first(passes[3])
            deviations()

            for i in range(2):
                copy_pairs(xT, D, *(s_xT[2] if i == 0 else s_hT), first=0)
                for b in range(5):
                    act.wait_ge(s_qk[i][0], b + 1)
                    A(qf[:, 5 * b * NV:5 * (b + 1) * NV], banks(2 + b % 2)[:, 0:5 * NV], ACT.Copy,
                      scale=float(D) ** -0.5).then_inc(s_qk[i][1], 1)
                attention(passes[3 + i])
                if i == 0:
                    prepare_first(passes[4])
                copy_pairs(qT, NV, *s_oT[i], first=0)
                for b in range(5):
                    act.wait_ge(s_y[i][0], b + 1)
                    A(Wk2[:, 5 * b:5 * b + 5, :], banks(4 + b % 2)[:, 0:5 * D].rearrange("p (t f) -> p t f", f=D),
                      ACT.Relu if i == 0 else ACT.Copy).then_inc(s_y[i][1], 1)
            deviations()

        @block.vector
        def _(dve):
            V = nc.vector
            steps = [0]

            def link(instruction):
                steps[0] += 1
                instruction.then_inc(s_dch, 1)
                dve.wait_ge(s_dch, steps[0])

            outv = OUT[:, :].rearrange("p (t f) -> p t f", f=NV)

            dve.wait_ge(s_iota, 1)
            V.tensor_copy(iota[:, :], iota_i[:, :])
            V.tensor_copy(part[:, :], part_i[:, :])
            V.tensor_copy(gnum[:, :], gnum_i[:, :])
            V.memset(X[:, NT - 1, :], 0.0).then_inc(s_X, 1)
            V.memset(ones[:, :], 1.0)
            V.memset(zrow[:, :], 0.0)
            V.memset(masked_b[:, :], -MASKED)
            V.memset(hid[:, :, :, :, D:D + 1], 0.0)
            V.tensor_copy(iota_h[:, :], iota_i[:, :])
            link(V.tensor_copy(vrow[:, :], vrow_i[:, :]))
            V.memset(hid[:, :, :, 0, D:D + 1], 1.0)
            V.tensor_scalar(before[:, :], iota[:, :], part[:, 0:1], None, ALU.is_gt)
            V.tensor_scalar(ident_h[:, :], iota[:, :], part[:, 0:1], None, ALU.is_equal)
            link(V.tensor_scalar(pick_at[:, :], iota[0:2 * G, 0:G], -2.0, part[0:2 * G, 0:1], ALU.mult, ALU.add))
            link(V.tensor_scalar(pick_at[:, :], pick_at[:, :], -0.5, None, ALU.add))
            link(V.tensor_tensor(pick_at[:, :], pick_at[:, :], pick_at[:, :], ALU.mult))
            V.tensor_scalar(pick[:, :, :], pick_at[:, :].unsqueeze(2).broadcast_to([2 * G, G, P]), 1.0, None, ALU.is_lt)
            V.tensor_scalar(ident[:, :], iota[:, :], part[:, 0:1], None, ALU.is_equal).then_inc(s_const, 1)

            def split(i):
                dve.wait_ge(s_key[i], 32)
                link(V.tensor_scalar(part_key_i[:, :], key_i[i][:, :], P - 1, None, ALU.bitwise_and))
                V.tensor_copy(key_f[i][:, :], key_i[i][:, :])
                link(V.tensor_copy(lo_f[i][:, :], part_key_i[:, :]))

            mask_r, csum_r = mask[:, 0:NB * RC], csum[:, 0:NB * RC]
            mask3, csum3 = (t.rearrange("p (v c) -> p v c", c=RC) for t in (mask_r, csum_r))

            def slots(i, q):
                cols = ds(q * RC, RC) if not isinstance(q, int) else slice(q * RC, (q + 1) * RC)
                next_slot, first = slot_at[:, 0, :], slot_at[:, 1, :]
                n = q * RANK_STEPS + i * (EC // RC * RANK_STEPS)

                def written(instruction, k):
                    instruction.then_inc(s_rank, 1)
                    dve.wait_ge(s_rank, n + k)
                    dve.nop(nofuse=True)
                written(V.tensor_tensor(mask3, hi_f[:, cols].unsqueeze(1).broadcast_to([EP, NB, RC]),
                                        vrow[0:EP, :].unsqueeze(2).broadcast_to([EP, NB, RC]), ALU.is_equal), 1)
                written(V.tensor_tensor_scan(csum_r, mask_r, zrow[0:EP, 0:1].broadcast_to([EP, NB * RC]), 0.0,
                                             ALU.add, ALU.max), 2)
                V.tensor_copy(first[:, 0:1], next_slot[:, 0:1]).then_inc(s_rank, 1)
                written(V.tensor_tensor(first[:, 1:NB], next_slot[:, 1:NB], csum3[:, 0:NB - 1, RC - 1], ALU.subtract), 4)
                V.tensor_tensor(next_slot, first, csum3[:, :, RC - 1], ALU.add).then_inc(s_rank, 1)
                dve.wait_ge(s_rank, n + 5)
                dve.nop(nofuse=True)
                written(V.tensor_tensor(csum3, csum3, first.unsqueeze(2).broadcast_to([EP, NB, RC]), ALU.add), 6)
                written(V.tensor_tensor(csum3, csum3, mask3, ALU.mult), 7)
                V.tensor_reduce(pos[i][:, cols], csum3.rearrange("p v c -> p c v"), AX.X, ALU.add).then_inc(s_rank, 1)
                dve.wait_ge(s_rank, n + RANK_STEPS)
                dve.sem_inc(s_pos[i], 1)

            def rank(i):
                link(V.tensor_scalar(part_key_i[:, :], key_i[i][:, :], P.bit_length() - 1, None, ALU.arith_shift_right))
                link(V.tensor_copy(hi_f[:, :], part_key_i[:, :]))
                for v in range(NT):
                    link(V.tensor_scalar(mask[:, :], hi_f[:, :], float(v), None, ALU.is_equal, ALU.add,
                                         accum_out=cnt[:, v:v + 1]))
                dve.sem_inc(s_cnt[i], 1)
                dve.wait_ge(s_pre[i], 1)
                link(V.tensor_scalar(srt[:, 0, :], banks(7)[:, 32:32 + NT], float(S - 1), None, ALU.add))
                link(V.tensor_copy(srt_i[:, :], srt[:, 0, :]))
                link(V.tensor_scalar(srt_i[:, :], srt_i[:, :], S.bit_length() - 1, None, ALU.arith_shift_right))
                link(V.tensor_copy(srt[:, 1, :], srt_i[:, :]))
                link(V.tensor_tensor_scan(srt[:, 2, :], srt[:, 1, :], zrow[:, :], 0.0, ALU.add, ALU.max))
                link(V.tensor_tensor(srt[:, 3, :], srt[:, 2, :], srt[:, 1, :], ALU.subtract))
                link(V.scalar_tensor_tensor(srt[:, 4, :], srt[:, 3, :], float(S), banks(7)[:, 0:NT], ALU.mult, ALU.add))
                V.memset(slot_at[:, 0, NT:NB], float(NG * S - 1))
                link(V.tensor_scalar(slot_at[:, 0, 0:NT], srt[:, 4, :], -1.0, None, ALU.add))
                slots(i, 0)
                with dve.Fori(1, EC // RC) as q:
                    slots(i, q)
                c3 = cmp.rearrange("p (g v) -> p g v", v=NT - 1)
                link(V.tensor_tensor(c3, srt[:, 3, 1:NT].unsqueeze(1).broadcast_to([P, NG, NT - 1]),
                                     gnum[:, :].unsqueeze(2).broadcast_to([P, NG, NT - 1]), ALU.is_le))
                link(V.tensor_reduce(bucket_f, c3, AX.X, ALU.add))
                V.tensor_copy(bucket[i][:, :], bucket_f[0:1, :]).then_inc(s_bkt[i], 1)
                V.memset(cap[i][:, 0:1], 0.0)
                link(V.tensor_tensor(cap[i][:, 1:NG], bucket_f[:, 1:NG], bucket_f[:, 0:NG - 1], ALU.is_equal))
                link(V.tensor_scalar(cap[i][:, 1:NG], cap[i][:, 1:NG], NO_BOUND, None, ALU.mult))
                link(V.tensor_scalar(cap[i][:, :], cap[i][:, :], NEW_BUCKET, None, ALU.add))

            def per_node(column):
                return column.unsqueeze(2).broadcast_to([P, NT, D])

            def moments(t=slice(0, NT)):
                n = t.stop - t.start

                def rows(column):
                    return column.unsqueeze(2).broadcast_to([P, n, D])
                link(V.tensor_reduce(stat[:, 0, t], Wk[:, t, :], AX.X, ALU.add))
                link(V.tensor_scalar(stat[:, 0, t], stat[:, 0, t], 1.0 / D, None, ALU.mult))
                link(V.tensor_tensor(Wk[:, t, :], Wk[:, t, :], rows(stat[:, 0, t]), ALU.subtract))
                link(V.tensor_tensor(Wk2[:, t, :], Wk[:, t, :], Wk[:, t, :], ALU.mult))
                link(V.tensor_reduce(stat[:, 1, t], Wk2[:, t, :], AX.X, ALU.add))
                last = V.tensor_scalar(stat[:, 2, t], stat[:, 1, t], 1.0 / D, LN_EPS, ALU.mult, ALU.add)
                if t.stop == NT:
                    last.then_inc(s_var, 1)

            def normalise():
                layer_norm.n += 1
                dve.wait_ge(s_std, layer_norm.n)
                link(V.reciprocal(stat[:, 0, :], stat[:, 3, :]))
                link(V.tensor_tensor(X[:, :, :], Wk[:, :, :], per_node(stat[:, 0, :]), ALU.mult))
                dve.sem_inc(s_X, 1)

            def layer_norm():
                moments()
                normalise()
            layer_norm.n = 0

            def split_nodes(rows_, width, ready=None, before=0):
                r = rows_.rearrange("p (t f) -> p t f", t=NT) if len(rows_.shape) == 2 else rows_
                n3 = node3[:, 0:NT * 3 * width].rearrange("p (t h f) -> p t h f", h=3, f=width)
                left = rest[:, 0:NT * width].rearrange("p (t f) -> p t f", t=NT)
                for b in range(5) if ready else (0,):
                    t = slice(5 * b, 5 * b + 5) if ready else slice(0, NT)
                    if ready:
                        dve.wait_ge(ready, before + b + 1)
                    link(V.tensor_copy(n3[:, t, 0, :], r[:, t, :]))
                    link(V.tensor_tensor(left[:, t, :], r[:, t, :], n3[:, t, 0, :], ALU.subtract))
                    link(V.tensor_copy(n3[:, t, 1, :], left[:, t, :]))
                    last = V.tensor_tensor(n3[:, t, 2, :], left[:, t, :], n3[:, t, 1, :], ALU.subtract)
                    if b == 4 or not ready:
                        last.then_inc(s_n3, 1)

            def clear(q, attention):
                if attention:
                    V.memset(ref_new[:, :], 0.0)
                    V.memset(faded[:, :, :], 0.0)
                link(V.memset(OUT[:, :], 0.0))

            def onehot(q, g):
                wait_done(dve, q.sum if q.i == 1 else q.ohw, g, back=SLOTS4)
                V.tensor_tensor(OH[:, g.ring, :, :], iota_h[:, :].unsqueeze(1).broadcast_to([P, G, P]),
                                q.meta[:, ds(g.k * G, G), q.m_lo].unsqueeze(2).broadcast_to([P, G, P]),
                                ALU.is_equal).then_inc(q.oh.sem, 1)

            def add_sums(q, g, width):
                b = bucket_of(dve, q, g)
                wait_done(dve, q.sum, g)
                wait_done(dve, q.acc, g, back=1)
                o = OUT[:, ds(b * NV, width)]
                V.tensor_tensor(o, o, banks(6 + g.par)[:, 0:width], ALU.add).then_inc(q.acc.sem, 1)

            def attention(q):
                def add_faded(g):
                    wait_done(dve, q.sum, g)
                    wait_done(dve, q.fade, g)
                    wait_done(dve, q.acc, g, back=1)
                    wait_done(dve, q.stored, g, back=2)
                    V.scalar_tensor_tensor(faded[:, g.par, :], faded[:, 1 - g.par, :], fade[:, g.ring:g.ring + 1],
                                           banks(6 + g.par)[:, 0:NV], ALU.mult, ALU.add).then_inc(q.acc.sem, 1)

                def maxima(g):
                    pm = slice(g.par, g.par + 1)
                    wait_done(dve, q.ro, g)
                    wait_done(dve, q.spread, g)
                    wait_done(dve, q.pen, g)
                    wait_done(dve, q.mn, g, back=1)
                    dve.nop(nofuse=True)
                    V.tensor_tensor_reduce(out=sm, in0=banks(4 + g.par), in1=pen[:, g.par, :],
                                           scale=1.0, scalar=ref_old[:, pm], op0=ALU.add, op1=ALU.max,
                                           accum_out=max_new[:, pm]).then_inc(q.mn.sem, 1)

                def products(g):
                    wait_ring(dve, s_gather, q.i, g, G)
                    if q.i:
                        wait_done(dve, q.acol, g)
                    wait_done(dve, q.qg, g)
                    wait_done(dve, q.score, g, back=2)
                    V.tensor_tensor(prod[:, g.par, 0:G * q.K].rearrange("p (j f) -> p j f", j=G),
                                    banks(0)[:, 0:G * q.K].rearrange("p (j f) -> p j f", j=G),
                                    xg[:, g.ring, :, q.key0:q.key0 + q.K], ALU.mult).then_inc(q.prod.sem, 1)

                def ref_head(g):
                    wait_done(dve, q.mn, g)
                    wait_done(dve, q.rg, g, back=2)
                    wait_done(dve, q.rn, g, back=2)
                    V.tensor_copy(ref2[:, g.par, 0:1], max_new[:, g.par:g.par + 1]).then_inc(q.r_hi.sem, 1)

                def scores(g):
                    wait_done(dve, q.prod, g)
                    wait_done(dve, q.less, g, back=2)
                    V.tensor_reduce(score[:, g.par, :], prod[:, g.par, 0:G * q.K].rearrange("p (j f) -> p j f", j=G),
                                    AX.X, ALU.add).then_inc(q.score.sem, 1)

                def ref_tail(g):
                    wait_done(dve, q.r_hi, g)
                    V.tensor_tensor(ref2[:, g.par, 1:2], max_new[:, g.par:g.par + 1], ref2[:, g.par, 0:1],
                                    ALU.subtract).then_inc(q.r2.sem, 1)

                def score_head(g):
                    wait_done(dve, q.score, g)
                    wait_done(dve, q.sT, g, back=2)
                    V.tensor_copy(score2[:, g.par, :, 0], score[:, g.par, :]).then_inc(q.s_hi.sem, 1)

                def reference(g):
                    wait_done(dve, q.r2, g)
                    wait_done(dve, q.fade, g, back=2)
                    wait_done(dve, q.ro, g, back=1)
                    V.tensor_tensor(ref_new[:, g.par:g.par + 1], ref2[:, g.par, 0:1], ref2[:, g.par, 1:2],
                                    ALU.add).then_inc(q.rn.sem, 1)

                def score_tail(g):
                    wait_done(dve, q.s_hi, g)
                    V.tensor_tensor(score2[:, g.par, :, 1], score[:, g.par, :], score2[:, g.par, :, 0],
                                    ALU.subtract).then_inc(q.s2.sem, 1)

                def old_reference(g):
                    wait_done(dve, q.rn, g, back=1)
                    wait_done(dve, q.fade, g, back=2)
                    dve.nop(nofuse=True)
                    V.tensor_scalar(ref_old[:, g.par:g.par + 1], ref_new[:, 1 - g.par:2 - g.par],
                                    cap[q.key][:, ds(g.k, 1)], None, ALU.min).then_inc(q.ro.sem, 1)

                def subtract_reference(g):
                    wait_done(dve, q.rg, g)
                    wait_done(dve, q.w, g, back=2)
                    V.tensor_tensor(less[:, g.par, :], score[:, g.par, :], banks(3)[:, 0:G], ALU.subtract)\
                        .then_inc(q.less.sem, 1)

                def weighted_onehot(g):
                    wait_done(dve, q.w, g)
                    wait_done(dve, q.sum, g, back=SLOTS4)
                    V.tensor_tensor(OHW[:, g.ring, :].rearrange("p (j n) -> p j n", j=G), OH[:, g.ring, :, :],
                                    wgt[:, g.par, :].unsqueeze(2).broadcast_to([P, G, P]), ALU.mult)\
                        .then_inc(q.ohw.sem, 1)

                def step(at):
                    if at(-1):
                        maxima(at(-1))
                    if at(0):
                        products(at(0))
                    if at(-1):
                        ref_head(at(-1))
                    if at(0):
                        scores(at(0))
                    if at(-1):
                        ref_tail(at(-1))
                    if at(0):
                        score_head(at(0))
                    if at(-1):
                        reference(at(-1))
                    if at(0):
                        score_tail(at(0))
                    if at(0):
                        old_reference(at(0))
                    if at(2):
                        onehot(q, at(2))
                    if at(-1):
                        subtract_reference(at(-1))
                    if at(-3):
                        add_faded(at(-3))
                    if at(-1):
                        weighted_onehot(at(-1))
                sweep(dve, step)
                done(q.stored, dve)
                link(V.tensor_scalar(stat[:, 0, :], outv[:, :, NV - 1], 1e-30, None, ALU.max))
                link(V.reciprocal(stat[:, 1, :], stat[:, 0, :]))

            split(1)
            split(0)
            rank(0)
            V.memset(xT[D:D + 1, :], 1.0)
            V.memset(mT[D:D + 1, :], 1.0)
            dve.wait_ge(s_x, 32)
            link(V.tensor_tensor(Wk[:, :, :], X[:, :, :], X[:, :, :], ALU.mult))
            V.tensor_reduce(stat[:, 0, :], Wk[:, :, :], AX.X, ALU.add).then_inc(s_sq, 1)
            dve.wait_ge(s_rel, 96)
            link(V.tensor_copy(rel_f[:, :], rel_i[:, :]))
            link(V.scalar_tensor_tensor(rel_f[:, :], rel_f[:, :], float(NPAD), key_f[0][:, :], ALU.mult, ALU.add))
            rank(1)

            dve.wait_ge(s_nrm, 1)
            link(V.tensor_scalar(stat[:, 2, :], stat[:, 1, :], NORM_EPS, None, ALU.max))
            link(V.reciprocal(stat[:, 0, :], stat[:, 2, :]))
            xn = big[:, 0:NT * 2 * D].rearrange("p (t f) -> p t f", f=2 * D)
            V.tensor_tensor(xn[:, :, 0:D], X[:, :, :], per_node(stat[:, 0, :]), ALU.mult)
            link(V.tensor_copy(xn[:, :, D:2 * D], X[:, :, :]))
            dve.sem_inc(s_hn, 1)
            split_nodes(xn[:, :, 0:D], D)

            dve.wait_ge(s_wts, 16 * len(WEIGHTS))
            for i in range(2):
                dve.wait_ge(s_wqT[0], i + 1)
                V.tensor_copy(wqT[:, i, 0:D], banks(4 + i)[0:D, 0:D]).then_inc(s_wqT[1], 1)
                V.tensor_copy(wqT[:, i, D:D + 1], bq_t[i][:, :]).then_inc(s_wqT[1], 1)
            for i in range(2):
                dve.wait_ge(s_fold[0], i + 1)
                V.tensor_copy(ka_t[i][:, :], banks(2 + i)[0:D + 1, 0:NV]).then_inc(s_fold[1], 1)

            def split_features(q, last):
                for j in range(NSC):
                    dve.wait_ge(s_at[j], q * 16 + 16)
                    if last:
                        dve.wait_ge(s_last[j], q * 16 + 16)
                    if not isinstance(q, int):
                        dve.wait_ge(s_sc[1][j], q * (16 * CB))
                        dve.nop(nofuse=True)
                    a = attr_in[:, j, :].rearrange("p (c f) -> p c f", f=FE)
                    r = row1[:, j, :].bitcast(bf16).rearrange("p (c f) -> p c f", f=2 * RF)
                    n = (q * NSC + j) * 3
                    V.tensor_copy(r[:, :, 0:FE], a).then_inc(s_spc, 1)
                    dve.wait_ge(s_spc, n + 1)
                    V.tensor_tensor(a, a, r[:, :, 0:FE], ALU.subtract).then_inc(s_spc, 1)
                    dve.wait_ge(s_spc, n + 2)
                    V.tensor_copy(r[:, :, FE:2 * FE], a).then_inc(s_spc, 1)
                    dve.wait_ge(s_spc, n + 3)
                    V.tensor_tensor(r[:, :, 2 * FE:3 * FE], a, r[:, :, FE:2 * FE], ALU.subtract).then_inc(s_split, 1)
            split_features(0, True)
            with dve.Fori(1, LAST_ROUNDS) as q:
                split_features(q, True)
            with dve.Fori(LAST_ROUNDS, NBLK // NSC) as q:
                split_features(q, False)

            dve.wait_ge(s_wts, 16 * len(WEIGHTS))
            link(V.tensor_copy(w1e_3[:, 0, :], w1e_t[:, :]))
            link(V.tensor_tensor(w1e_r[:, :], w1e_t[:, :], w1e_3[:, 0, :], ALU.subtract))
            link(V.tensor_copy(w1e_3[:, 1, :], w1e_r[:, :]))
            link(V.tensor_tensor(w1e_3[:, 2, :], w1e_r[:, :], w1e_3[:, 1, :], ALU.subtract))
            clear(passes[0], True)
            dve.wait_ge(s_meta[0], META_LOADS[0])
            dve.wait_ge(s_fillt, 5)
            attention(passes[0])
            link(V.tensor_tensor(Wk[:, :, :], outv[:, :, 0:D], per_node(stat[:, 1, :]), ALU.mult))
            link(V.tensor_tensor(Wk[:, :, :], Wk[:, :, :], X[:, :, :], ALU.add))
            layer_norm()

            q1 = passes[1]
            clear(q1, False)
            dve.wait_ge(s_meta[1], META_LOADS[1])

            split_nodes(Bt, D, s_A[1], 5)

            def rows_of(t, g):
                return t[:, g.par, :].rearrange("p (j f) -> p j f", f=D)

            def add_source(g):
                wait_ring(dve, s_gather, 1, g, G)
                wait_done(dve, q1.hidden, g)
                wait_done(dve, q1.hi, g, back=2)
                wait_done(dve, q1.rest, g, back=2)
                V.tensor_tensor(rows_of(hsum, g), banks(2 + g.par)[:, 0:G * D].rearrange("p (j f) -> p j f", f=D),
                                xg[:, g.ring, :, VAL:VAL + D], ALU.add).then_inc(q1.hsum.sem, 1)

            def leave(g):
                wait_done(dve, q1.hi, g)
                wait_done(dve, q1.lo, g, back=2)
                V.scalar_tensor_tensor(rows_of(hres, g), rows_of(hsum, g), 0.0, hid[:, g.par, :, 0, 0:D],
                                       ALU.max, ALU.subtract).then_inc(q1.rest.sem, 1)

            def tail(g):
                wait_done(dve, q1.mid, g)
                V.tensor_tensor(hid[:, g.par, :, 2, 0:D], rows_of(hres, g), hid[:, g.par, :, 1, 0:D],
                                ALU.subtract).then_inc(q1.lo.sem, 1)

            def step(at):
                if at(0):
                    add_source(at(0))
                if at(2):
                    onehot(q1, at(2))
                if at(0):
                    leave(at(0))
                if at(-2):
                    add_sums(q1, at(-2), D + 1)
                if at(0):
                    tail(at(0))
            sweep(dve, step)
            for b in range(5):
                t = slice(5 * b, 5 * b + 5)
                dve.wait_ge(s_gate[1], 2 * (b + 1))
                link(V.tensor_tensor(Wk[:, t, :], gates[:, t, 0:D], gates[:, t, 3 * D:4 * D], ALU.mult))
                V.tensor_tensor(Wk[:, t, :], Wk[:, t, :], gates[:, t, 2 * D:3 * D], ALU.add).then_inc(s_cand, 1)
                dve.wait_ge(s_tanh, b + 1)
                link(V.tensor_tensor(Wk[:, t, :], X[:, t, :], Wk2[:, t, :], ALU.subtract))
                link(V.tensor_tensor(Wk[:, t, :], Wk[:, t, :], gates[:, t, D:2 * D], ALU.mult))
                link(V.tensor_tensor(Wk[:, t, :], Wk[:, t, :], Wk2[:, t, :], ALU.add))
                link(V.tensor_tensor(Wk[:, t, :], Wk[:, t, :], X[:, t, :], ALU.add))
                moments(t)
            normalise()

            q2 = passes[2]
            clear(q2, False)

            def weighted(g):
                wait_done(dve, q2.sum, g, back=SLOTS4)
                for j in range(G):
                    e = ds(g.k * G + j, 1)
                    last = V.tensor_scalar(OHW[:, g.ring, tile(j)], iota[:, :], meta1[:, e, M_LO], meta1[:, e, M_W],
                                           ALU.is_equal, ALU.mult)
                last.then_inc(q2.oh.sem, 1)

            def step(at):
                if at(-1):
                    add_sums(q2, at(-1), D)
                if at(1):
                    weighted(at(1))
            sweep(dve, step)
            done(q2.acc, dve)
            link(V.tensor_tensor(Wk[:, :, :], outv[:, :, 0:D], X[:, :, :], ALU.add))
            layer_norm()

            for i in range(2):
                if i == 1:
                    dve.wait_ge(s_oT[0][0], 5)
                clear(passes[3 + i], True)
                split_nodes(qf, NV, s_qk[i][1])
                attention(passes[3 + i])
                V.tensor_tensor(outv, outv, stat[:, 1, :].unsqueeze(2).broadcast_to([P, NT, NV]), ALU.mult)\
                    .then_inc(s_on[i], 1)
            for b in range(5):
                t = slice(5 * b, 5 * b + 5)
                dve.wait_ge(s_y[1][1], b + 1)
                link(V.tensor_tensor(Wk[:, t, :], Wk2[:, t, :], X[:, t, :], ALU.add))
                moments(t)
            normalise()


def kernel(**inputs):
    import numpy as _np
    import concourse.bacc as _bacc
    from concourse import mybir as _mybir
    from concourse.bass_utils import run_bass_kernel_spmd as _run

    a = {k: _np.asarray(v) for k, v in inputs.items()}
    w1 = a["L1_gnn_W1"]
    arrays = {
        "x": a["x"], "src": a["src"], "dst": a["dst"], "attr": a["edge_attr_32"], "etype": a["edge_type_8"],
        "ew": a["edge_weight"], "ew1": a["edge_weight1"],
        "w1s": w1[:, 0:D].T, "w1d": _np.concatenate([w1[:, D:2 * D].T, a["L1_gnn_b1"][None]]),
        "w1e": w1[:, 2 * D:].T, "w2b": _np.concatenate([a["L1_gnn_W2"].T, a["L1_gnn_b2"][None]]),
        "wi": _np.concatenate([a["L1_gnn_w_ih"].T, a["L1_gnn_b_ih"][None]]),
        "wh": _np.concatenate([a["L1_gnn_w_hh"].T, a["L1_gnn_b_hh"][None]]),
        "xw_w": a["L2_gnn_W"].transpose(1, 0, 2).reshape(D, RELS * D),
    }
    for i in ("1", "2"):
        w = {k: a[f"L3_gnn_{k}{i}"] for k in ("Wq", "bq", "Wk", "bk", "Wv", "bv", "We", "Ws", "bs")}
        arrays["wq" + i] = w["Wq"]
        arrays["bq" + i] = w["bq"][:, None]
        arrays["ka" + i] = _np.concatenate([w["Wk"].T, w["We"].T, w["bk"][:, None]], axis=1)
        arrays["wva" + i] = _np.concatenate([w["Wv"], w["We"], w["bv"][None]])
        arrays["wsa" + i] = _np.concatenate([w["Ws"], w["bs"][None]])
    arrays = {f"in_{k}_dram": _np.ascontiguousarray(v) for k, v in arrays.items()}

    nc = _bacc.Bacc("TRN2", target_bir_lowering=False, num_devices=1)
    p = {k[3:-5]: nc.dram_tensor(k, v.shape, _mybir.dt.from_np(v.dtype), kind="ExternalInput").ap()
         for k, v in arrays.items()}
    f32 = _mybir.dt.float32
    out = nc.dram_tensor("out_dram", (NODES, D), f32, kind="ExternalOutput").ap()
    scratch = [nc.dram_tensor(n, s, f32, kind=SCRATCH_KIND).ap() for n, s in (
        ("edges_by_source", (NSLOT, R0)), ("edges_by_destination", (NSLOT, RF)), ("unit_nodes", (NPAD, 2 * D)),
        ("source_part", (NPAD, D)), ("relation_nodes", (RELS * NPAD, D)), ("conv1_nodes", (NPAD, D)),
        ("conv2_nodes", (NPAD, D)))]
    gnn_kernel(nc, *(p[k] for k in ("x", "src", "dst", "attr", "etype", "ew", "ew1", "w1s", "w1d", "w1e",
                                    "w2b", "wi", "wh", "xw_w")),
               *([p[k + "1"], p[k + "2"]] for k in ("wq", "bq", "ka", "wva", "wsa")), out, scratch)
    r = _run(nc, [arrays], core_ids=[0])
    return r.results[0]["out_dram"]
```
